# Optimizing a Trainium2 kernel written in Bass

```python
import numpy as np
import jax
import jax.numpy as jnp

def _softmax(x, axis=-1):
    return jax.nn.softmax(x, axis=axis)

def _gelu(x):
    return jax.nn.gelu(x, approximate=True)

def _silu(x):
    return jax.nn.silu(x)

def _sigmoid(x):
    return jax.nn.sigmoid(x)

def _layernorm(x, axis=-1, eps=1e-05):
    m = jnp.mean(x, axis=axis, keepdims=True)
    v = jnp.var(x, axis=axis, keepdims=True)
    return (x - m) / jnp.sqrt(v + eps)

def _scatter_add(tgt, idx, src, axis=0):
    return tgt.at[idx].add(src)

def _segment_sum(src, seg, n):
    return jax.ops.segment_sum(src, seg, n)
kernel_name = 'mk_dlrm_tower_d1_rec_r8_a2801a'

def setup_inputs(seed: int=0):
    np.random.seed(seed)
    _w = jnp.asarray

    def _rec_inputs():
        import jax
        import jax.numpy as jnp
        _tk = jax.random.key(seed)
        dense_ctx = jax.random.normal(jax.random.fold_in(_tk, 190), (512, 16), jnp.float32)
        ids = jnp.stack([jax.random.randint(jax.random.fold_in(_tk, 200 + f), (512,), 0, v, jnp.int32) for f, v in enumerate([1250, 1000, 125000, 1250, 1250, 125000, 125000, 125000, 125000, 1250, 1250, 12500, 12500, 1000, 1000, 12500, 1250, 1250, 12500, 12500, 12500, 1250, 12500, 125000, 125000, 1250, 125000, 1250, 12500, 1000, 125000, 125000, 12500, 1000, 125000, 1000, 1250, 1250, 12500])], axis=1)
        tbl_0 = 0.05 * jax.random.normal(jax.random.fold_in(_tk, 500 + 0), (1250, 16), jnp.float32)
        tbl_1 = 0.05 * jax.random.normal(jax.random.fold_in(_tk, 500 + 1), (1000, 16), jnp.float32)
        tbl_2 = 0.05 * jax.random.normal(jax.random.fold_in(_tk, 500 + 2), (125000, 16), jnp.float32)
        tbl_3 = 0.05 * jax.random.normal(jax.random.fold_in(_tk, 500 + 3), (1250, 16), jnp.float32)
        tbl_4 = 0.05 * jax.random.normal(jax.random.fold_in(_tk, 500 + 4), (1250, 16), jnp.float32)
        tbl_5 = 0.05 * jax.random.normal(jax.random.fold_in(_tk, 500 + 5), (125000, 16), jnp.float32)
        tbl_6 = 0.05 * jax.random.normal(jax.random.fold_in(_tk, 500 + 6), (125000, 16), jnp.float32)
        tbl_7 = 0.05 * jax.random.normal(jax.random.fold_in(_tk, 500 + 7), (125000, 16), jnp.float32)
        tbl_8 = 0.05 * jax.random.normal(jax.random.fold_in(_tk, 500 + 8), (125000, 16), jnp.float32)
        tbl_9 = 0.05 * jax.random.normal(jax.random.fold_in(_tk, 500 + 9), (1250, 16), jnp.float32)
        tbl_10 = 0.05 * jax.random.normal(jax.random.fold_in(_tk, 500 + 10), (1250, 16), jnp.float32)
        tbl_11 = 0.05 * jax.random.normal(jax.random.fold_in(_tk, 500 + 11), (12500, 16), jnp.float32)
        tbl_12 = 0.05 * jax.random.normal(jax.random.fold_in(_tk, 500 + 12), (12500, 16), jnp.float32)
        tbl_13 = 0.05 * jax.random.normal(jax.random.fold_in(_tk, 500 + 13), (1000, 16), jnp.float32)
        tbl_14 = 0.05 * jax.random.normal(jax.random.fold_in(_tk, 500 + 14), (1000, 16), jnp.float32)
        tbl_15 = 0.05 * jax.random.normal(jax.random.fold_in(_tk, 500 + 15), (12500, 16), jnp.float32)
        tbl_16 = 0.05 * jax.random.normal(jax.random.fold_in(_tk, 500 + 16), (1250, 16), jnp.float32)
        tbl_17 = 0.05 * jax.random.normal(jax.random.fold_in(_tk, 500 + 17), (1250, 16), jnp.float32)
        tbl_18 = 0.05 * jax.random.normal(jax.random.fold_in(_tk, 500 + 18), (12500, 16), jnp.float32)
        tbl_19 = 0.05 * jax.random.normal(jax.random.fold_in(_tk, 500 + 19), (12500, 16), jnp.float32)
        tbl_20 = 0.05 * jax.random.normal(jax.random.fold_in(_tk, 500 + 20), (12500, 16), jnp.float32)
        tbl_21 = 0.05 * jax.random.normal(jax.random.fold_in(_tk, 500 + 21), (1250, 16), jnp.float32)
        tbl_22 = 0.05 * jax.random.normal(jax.random.fold_in(_tk, 500 + 22), (12500, 16), jnp.float32)
        tbl_23 = 0.05 * jax.random.normal(jax.random.fold_in(_tk, 500 + 23), (125000, 16), jnp.float32)
        tbl_24 = 0.05 * jax.random.normal(jax.random.fold_in(_tk, 500 + 24), (125000, 16), jnp.float32)
        tbl_25 = 0.05 * jax.random.normal(jax.random.fold_in(_tk, 500 + 25), (1250, 16), jnp.float32)
        tbl_26 = 0.05 * jax.random.normal(jax.random.fold_in(_tk, 500 + 26), (125000, 16), jnp.float32)
        tbl_27 = 0.05 * jax.random.normal(jax.random.fold_in(_tk, 500 + 27), (1250, 16), jnp.float32)
        tbl_28 = 0.05 * jax.random.normal(jax.random.fold_in(_tk, 500 + 28), (12500, 16), jnp.float32)
        tbl_29 = 0.05 * jax.random.normal(jax.random.fold_in(_tk, 500 + 29), (1000, 16), jnp.float32)
        tbl_30 = 0.05 * jax.random.normal(jax.random.fold_in(_tk, 500 + 30), (125000, 16), jnp.float32)
        tbl_31 = 0.05 * jax.random.normal(jax.random.fold_in(_tk, 500 + 31), (125000, 16), jnp.float32)
        tbl_32 = 0.05 * jax.random.normal(jax.random.fold_in(_tk, 500 + 32), (12500, 16), jnp.float32)
        tbl_33 = 0.05 * jax.random.normal(jax.random.fold_in(_tk, 500 + 33), (1000, 16), jnp.float32)
        tbl_34 = 0.05 * jax.random.normal(jax.random.fold_in(_tk, 500 + 34), (125000, 16), jnp.float32)
        tbl_35 = 0.05 * jax.random.normal(jax.random.fold_in(_tk, 500 + 35), (1000, 16), jnp.float32)
        tbl_36 = 0.05 * jax.random.normal(jax.random.fold_in(_tk, 500 + 36), (1250, 16), jnp.float32)
        tbl_37 = 0.05 * jax.random.normal(jax.random.fold_in(_tk, 500 + 37), (1250, 16), jnp.float32)
        tbl_38 = 0.05 * jax.random.normal(jax.random.fold_in(_tk, 500 + 38), (12500, 16), jnp.float32)
        _rk = jax.random.fold_in(_tk, 7)
        W_top1 = 0.0606339 * jax.random.normal(jax.random.fold_in(_tk, 801), (272, 512), jnp.float32)
        W_top2 = 0.0441942 * jax.random.normal(jax.random.fold_in(_tk, 802), (512, 256), jnp.float32)
        W_top3 = 0.0625 * jax.random.normal(jax.random.fold_in(_tk, 803), (256, 1), jnp.float32)
        b_top1 = jnp.zeros((512,), jnp.float32)
        b_top2 = jnp.zeros((256,), jnp.float32)
        return (dense_ctx, ids, tbl_0, tbl_1, tbl_2, tbl_3, tbl_4, tbl_5, tbl_6, tbl_7, tbl_8, tbl_9, tbl_10, tbl_11, tbl_12, tbl_13, tbl_14, tbl_15, tbl_16, tbl_17, tbl_18, tbl_19, tbl_20, tbl_21, tbl_22, tbl_23, tbl_24, tbl_25, tbl_26, tbl_27, tbl_28, tbl_29, tbl_30, tbl_31, tbl_32, tbl_33, tbl_34, tbl_35, tbl_36, tbl_37, tbl_38, W_top1, b_top1, W_top2, b_top2, W_top3)
    dense_ctx, ids, tbl_0, tbl_1, tbl_2, tbl_3, tbl_4, tbl_5, tbl_6, tbl_7, tbl_8, tbl_9, tbl_10, tbl_11, tbl_12, tbl_13, tbl_14, tbl_15, tbl_16, tbl_17, tbl_18, tbl_19, tbl_20, tbl_21, tbl_22, tbl_23, tbl_24, tbl_25, tbl_26, tbl_27, tbl_28, tbl_29, tbl_30, tbl_31, tbl_32, tbl_33, tbl_34, tbl_35, tbl_36, tbl_37, tbl_38, W_top1, b_top1, W_top2, b_top2, W_top3 = _rec_inputs()

    def _L0_rec_setup():
        import jax, jax.numpy as jnp
        import numpy as np
        B, F0, D = (256, 39, 16)
        LAYER_SIZES = [128, 128, 128]
        key = jax.random.key(seed)
        ks = jax.random.split(key, 1 + 2 * len(LAYER_SIZES))
        inputs = jax.random.normal(ks[0], (B, F0, D), dtype=jnp.float32)
        out = {'inputs': inputs}
        field_nums = [F0]
        for i, size in enumerate(LAYER_SIZES):
            fk = field_nums[-1]
            fan_in = F0 * fk
            scale = np.sqrt(2.0 / (fan_in + size)).astype(np.float32)
            out[f'w{i}'] = jax.random.normal(ks[1 + 2 * i], (F0, fk, size), dtype=jnp.float32) * scale
            out[f'b{i}'] = jnp.zeros((size,), dtype=jnp.float32)
            field_nums.append(size // 2)
        return out
    _L0_rec_all = _L0_rec_setup()
    _L0_rec_in = {k: v for k, v in _L0_rec_all.items() if k in ('w0', 'w1', 'w2', 'b0', 'b1', 'b2')}
    del _L0_rec_all
    return {'dense_ctx': dense_ctx, 'ids': ids, 'tbl_0': tbl_0, 'tbl_1': tbl_1, 'tbl_2': tbl_2, 'tbl_3': tbl_3, 'tbl_4': tbl_4, 'tbl_5': tbl_5, 'tbl_6': tbl_6, 'tbl_7': tbl_7, 'tbl_8': tbl_8, 'tbl_9': tbl_9, 'tbl_10': tbl_10, 'tbl_11': tbl_11, 'tbl_12': tbl_12, 'tbl_13': tbl_13, 'tbl_14': tbl_14, 'tbl_15': tbl_15, 'tbl_16': tbl_16, 'tbl_17': tbl_17, 'tbl_18': tbl_18, 'tbl_19': tbl_19, 'tbl_20': tbl_20, 'tbl_21': tbl_21, 'tbl_22': tbl_22, 'tbl_23': tbl_23, 'tbl_24': tbl_24, 'tbl_25': tbl_25, 'tbl_26': tbl_26, 'tbl_27': tbl_27, 'tbl_28': tbl_28, 'tbl_29': tbl_29, 'tbl_30': tbl_30, 'tbl_31': tbl_31, 'tbl_32': tbl_32, 'tbl_33': tbl_33, 'tbl_34': tbl_34, 'tbl_35': tbl_35, 'tbl_36': tbl_36, 'tbl_37': tbl_37, 'tbl_38': tbl_38, 'W_top1': W_top1, 'b_top1': b_top1, 'W_top2': W_top2, 'b_top2': b_top2, 'W_top3': W_top3, 'L0_rec_w0': _L0_rec_in['w0'], 'L0_rec_w1': _L0_rec_in['w1'], 'L0_rec_w2': _L0_rec_in['w2'], 'L0_rec_b0': _L0_rec_in['b0'], 'L0_rec_b1': _L0_rec_in['b1'], 'L0_rec_b2': _L0_rec_in['b2']}

def reference(dense_ctx, ids, tbl_0, tbl_1, tbl_2, tbl_3, tbl_4, tbl_5, tbl_6, tbl_7, tbl_8, tbl_9, tbl_10, tbl_11, tbl_12, tbl_13, tbl_14, tbl_15, tbl_16, tbl_17, tbl_18, tbl_19, tbl_20, tbl_21, tbl_22, tbl_23, tbl_24, tbl_25, tbl_26, tbl_27, tbl_28, tbl_29, tbl_30, tbl_31, tbl_32, tbl_33, tbl_34, tbl_35, tbl_36, tbl_37, tbl_38, W_top1, b_top1, W_top2, b_top2, W_top3, L0_rec_w0, L0_rec_w1, L0_rec_w2, L0_rec_b0, L0_rec_b1, L0_rec_b2):
    import jax
    import jax.numpy as jnp

    def _L0_rec_ref(inputs, w0, w1, w2, b0, b1, b2):
        import jax, jax.numpy as jnp
        import numpy as np
        B, F0, D = (256, 39, 16)
        LAYER_SIZES = [128, 128, 128]
        x0 = inputs
        xk = inputs
        params = [(w0, b0), (w1, b1), (w2, b2)]
        n_layers = len(params)
        direct = []
        for idx, (W, b) in enumerate(params):
            z = jnp.einsum('bhd,bkd,hks->bsd', x0, xk, W) + b[None, :, None]
            z = jax.nn.relu(z)
            if idx != n_layers - 1:
                half = z.shape[1] // 2
                xk = z[:, :half, :]
                direct.append(z[:, half:, :])
            else:
                direct.append(z)
        logit = jnp.sum(jnp.concatenate(direct, axis=1), axis=-1)
        return logit
    e = jnp.stack([tbl_0[ids[:, 0]], tbl_1[ids[:, 1]], tbl_2[ids[:, 2]], tbl_3[ids[:, 3]], tbl_4[ids[:, 4]], tbl_5[ids[:, 5]], tbl_6[ids[:, 6]], tbl_7[ids[:, 7]], tbl_8[ids[:, 8]], tbl_9[ids[:, 9]], tbl_10[ids[:, 10]], tbl_11[ids[:, 11]], tbl_12[ids[:, 12]], tbl_13[ids[:, 13]], tbl_14[ids[:, 14]], tbl_15[ids[:, 15]], tbl_16[ids[:, 16]], tbl_17[ids[:, 17]], tbl_18[ids[:, 18]], tbl_19[ids[:, 19]], tbl_20[ids[:, 20]], tbl_21[ids[:, 21]], tbl_22[ids[:, 22]], tbl_23[ids[:, 23]], tbl_24[ids[:, 24]], tbl_25[ids[:, 25]], tbl_26[ids[:, 26]], tbl_27[ids[:, 27]], tbl_28[ids[:, 28]], tbl_29[ids[:, 29]], tbl_30[ids[:, 30]], tbl_31[ids[:, 31]], tbl_32[ids[:, 32]], tbl_33[ids[:, 33]], tbl_34[ids[:, 34]], tbl_35[ids[:, 35]], tbl_36[ids[:, 36]], tbl_37[ids[:, 37]], tbl_38[ids[:, 38]]], axis=1)
    z = _L0_rec_ref(e, L0_rec_w0, L0_rec_w1, L0_rec_w2, L0_rec_b0, L0_rec_b1, L0_rec_b2)
    z = z.reshape(z.shape[0], -1)
    h = jnp.concatenate([z, dense_ctx], axis=1)
    h = jnp.maximum(h @ W_top1 + b_top1, 0.0)
    h = jnp.maximum(h @ W_top2 + b_top2, 0.0)
    y = h @ W_top3
    return y

_drawn_inputs = setup_inputs


def setup_inputs(seed=0):
    import zlib

    import numpy as np

    out = dict(_drawn_inputs(seed))
    spreads = {'b_top1': (0.0, 2.0),
     'b_top2': (0.0, 2.0),
     'L0_rec_b0': (0.0, 0.345),
     'L0_rec_b1': (0.0, 0.572),
     'L0_rec_b2': (0.0, 0.8)}
    factors = {'tbl_0': 8.0,
     'tbl_1': 8.0,
     'tbl_2': 8.0,
     'tbl_3': 8.0,
     'tbl_4': 8.0,
     'tbl_5': 8.0,
     'tbl_6': 8.0,
     'tbl_7': 8.0,
     'tbl_8': 8.0,
     'tbl_9': 8.0,
     'tbl_10': 8.0,
     'tbl_11': 8.0,
     'tbl_12': 8.0,
     'tbl_13': 8.0,
     'tbl_14': 8.0,
     'tbl_15': 8.0,
     'tbl_16': 8.0,
     'tbl_17': 8.0,
     'tbl_18': 8.0,
     'tbl_19': 8.0,
     'tbl_20': 8.0,
     'tbl_21': 8.0,
     'tbl_22': 8.0,
     'tbl_23': 8.0,
     'tbl_24': 8.0,
     'tbl_25': 8.0,
     'tbl_26': 8.0,
     'tbl_27': 8.0,
     'tbl_28': 8.0,
     'tbl_29': 8.0,
     'tbl_30': 8.0,
     'tbl_31': 8.0,
     'tbl_32': 8.0,
     'tbl_33': 8.0,
     'tbl_34': 8.0,
     'tbl_35': 8.0,
     'tbl_36': 8.0,
     'tbl_37': 8.0,
     'tbl_38': 8.0,
     'L0_rec_w0': 8.0,
     'L0_rec_w1': 6.474,
     'L0_rec_w2': 4.746,
     'dense_ctx': 8.0}
    for name, (base, spread) in spreads.items():
        noise = np.random.default_rng([zlib.crc32(name.encode()), seed]).standard_normal(out[name].shape)
        drawn = base * np.exp(spread * noise) if base else spread * noise
        out[name] = jnp.asarray(drawn.astype(out[name].dtype))
    for name, factor in factors.items():
        out[name] = (out[name] * factor).astype(out[name].dtype)
    return out
```

```python
import numpy as np
import concourse.bass as bass
from concourse import mybir
from contextlib import ExitStack

B, F, D = 512, 39, 16
SIZES = [1250, 1000, 125000, 1250, 1250, 125000, 125000, 125000, 125000, 1250, 1250, 12500, 12500,
         1000, 1000, 12500, 1250, 1250, 12500, 12500, 12500, 1250, 12500, 125000, 125000, 1250,
         125000, 1250, 12500, 1000, 125000, 125000, 12500, 1000, 125000, 1000, 1250, 1250, 12500]
S, HALF = 128, 64
BC = 32
N = BC * D
C = B // BC
GR, GB = 3, 11
G0 = [0, GB, BC - GB]
GP = GR * F
SH = (F + 1) // 2
T0 = -(-SH // GR)
ROWS = F + SH - 1
T1 = -(-F // 2)
QT = T1 // 4
DENSE = 16
H1, H2 = 512, 256

RING = 16


def step(layer, tiles, partitions, position):
    groups, t = [], 0
    while t < tiles:
        n = 2 if t + 2 < tiles or (t + 2 == tiles and partitions[-1] == partitions[-2]) else 1
        groups.append((layer, t, n, partitions[t], position + t))
        t += n
    return groups


L1_GROUPS = step(1, T1, [S] * (T1 - 1) + [HALF], 0)
L0_GROUPS = step(0, T0, [GP] * (T0 - 1) + [(SH - GR * (T0 - 1)) * F], T1)
L2_AT = T1 + T0 + (T0 + T1) % 2
L2_GROUPS = step(2, T1, [S] * (T1 - 1) + [HALF], L2_AT)
BODY = L1_GROUPS + L0_GROUPS + L2_GROUPS
TURN = L2_AT + T1
assert TURN % RING == 0 and all(p % RING + n <= RING for _, _, n, _, p in BODY)
N1, N0 = len(L1_GROUPS), len(L0_GROUPS)
PER_BODY = len(BODY)


def groups_done(c, index):
    return N0 + PER_BODY * c + index + 1


def slot_free(c, group):
    _, _, n, _, position = group
    q, back = position + n - 1 - RING, 0
    if q < 0:
        q, back = q + TURN, 1
    index = max(i for i, g in enumerate(BODY) if g[4] <= q)
    if back and isinstance(c, int) and c == 0:
        return N0
    return groups_done(c - back, index)


def dlrm_cin_kernel(nc, ids, base, tables, dense, w0a, w0b, b0, bx0, w1, b1, bx1, w2, b2,
                    wt1, bt1, wt2, bt2, wt3, out):
    fp32, i32 = mybir.dt.float32, mybir.dt.int32
    ALU, ACT, AX = mybir.AluOpType, mybir.ActivationFunctionType, mybir.AxisListType
    RELU = ACT.Relu

    ctx = ExitStack()
    with ctx:
        def sb(name, shape, dt=fp32):
            return ctx.enter_context(nc.sbuf_tensor(name, shape, dt))

        def bank(name):
            return ctx.enter_context(nc.psum_tensor(name, [128, N], fp32))

        def sem(name):
            return ctx.enter_context(nc.semaphore(name))

        x0_rows = nc.dram_tensor("x0_rows", [C, ROWS, N], fp32, kind="Internal")

        ids_sb = sb("ids_sb", [GP, C * GB], i32)
        base_sb = sb("base_sb", [GP, 1], i32)
        rows_sb = sb("rows_sb", [GP, GB], i32)
        fence = sb("fence", [1, 1], i32)
        gathered = sb("gathered", [GP, GB * D])
        x0_same = sb("x0_same", [GP, N])
        x0_shifted = sb("x0_shifted", [GP, T0, N])
        x0_rep = sb("x0_rep", [128, 2 * T1, N])
        products = sb("products", [128, RING, N])
        w0_sb = sb("w0_sb", [GP, T0, S])
        w1_sb = sb("w1_sb", [128, T1, S])
        w2_sb = sb("w2_sb", [128, T1, S])
        b0_sb, bx0_sb = sb("b0_sb", [128, 1]), sb("bx0_sb", [128, 1])
        b1_sb, bx1_sb = sb("b1_sb", [128, 1]), sb("bx1_sb", [128, 1])
        b2_sb = sb("b2_sb", [128, 1])
        direct01 = sb("direct01", [128, N])
        direct2 = sb("direct2", [128, N])
        logit01 = sb("logit01", [128, B])
        logit2 = sb("logit2", [128, B])
        dense_sb = sb("dense_sb", [DENSE, B])
        wt1_sb = sb("wt1_sb", [128, 2, H1])
        wt1d_sb = sb("wt1d_sb", [DENSE, H1])
        wt2_sb = sb("wt2_sb", [128, H1 // 128, H2])
        wt3_sb = sb("wt3_sb", [128, H2 // 128])
        bt1_sb = sb("bt1_sb", [128, H1 // 128])
        bt2_sb = sb("bt2_sb", [128, H2 // 128])
        w0b_sb = products[0:GP, 0:2, :].rearrange("p a n -> p (a n)")[:, 0:T0 * S] \
            .rearrange("p (t s) -> p t s", s=S)
        w0a_sb = products[0:GP, 2:4, :].rearrange("p a n -> p (a n)")[:, 0:T0 * S] \
            .rearrange("p (t s) -> p t s", s=S)
        hidden1 = products[:, 0:4, :]
        hidden2 = products[:, 4:6, :]
        y_sb = products[0:1, 6, :]

        z = [bank("z0"), bank("z1"), bank("z2")]
        xk = [bank("xk0"), bank("xk1")]
        spare = [bank("spare0"), bank("spare1"), bank("spare2")]
        z_hidden1 = [spare[0], spare[1], spare[2], z[0]]
        z_hidden2 = [z[1], xk[0]]
        z_y = xk[1]

        ids_loaded = sem("ids_loaded")
        rows_made = sem("rows_made")
        gather_done = sem("gather_done")
        x0_written = sem("x0_written")
        w0_loaded = sem("w0_loaded")
        w0_added = sem("w0_added")
        w0_folded = sem("w0_folded")
        w1_loaded = sem("w1_loaded")
        w2_loaded = sem("w2_loaded")
        biases_loaded = sem("biases_loaded")
        top_loaded = sem("top_loaded")
        l0_loaded = sem("l0_loaded")
        rep_loaded = [sem(f"rep_loaded{q}") for q in range(4)]
        made = sem("made")
        used = sem("used")
        xk0_ready, xk1_ready = sem("xk0_ready"), sem("xk1_ready")
        direct0_ready, direct1_ready = sem("direct0_ready"), sem("direct1_ready")
        direct2_ready = sem("direct2_ready")
        logit01_ready, logit2_ready = sem("logit01_ready"), sem("logit2_ready")
        hidden1_done, hidden1_ready = sem("hidden1_done"), sem("hidden1_ready")
        hidden2_done, hidden2_ready = sem("hidden2_done"), sem("hidden2_ready")
        y_done, y_ready = sem("y_done"), sem("y_ready")
        stored = sem("stored")

        block = ctx.enter_context(nc.Block())
        WRITES = 2 * GR
        L0_LOADS = 2 * GR

        @block.sync
        def _(sp):
            def load_layer0(c):
                for r in range(GR):
                    n = T0 if GR * (T0 - 1) + r < SH else T0 - 1
                    sp.dma_start(x0_same[r * F:(r + 1) * F, :],
                                 x0_rows[bass.ds(c, 1), 0:F, :].rearrange("a k n -> (a k) n")).then_inc(l0_loaded, 16)
                    src = x0_rows[bass.ds(c, 1), r:r + F, :].rearrange("a k n -> (a k) n").unsqueeze(1)
                    src = bass.AP(src.tensor, src.offset, [[N, F], [GR * N, n], [1, N]])
                    sp.dma_start(x0_shifted[r * F:(r + 1) * F, 0:n, :], src).then_inc(l0_loaded, 16)

            def load_replicated(c, half):
                for q in range(4):
                    for e in range(2):
                        n = QT if 2 * (QT * (q + 1) - 1) + e < F else QT - 1
                        src = x0_rows[bass.ds(c, 1), 2 * QT * q + e:2 * QT * q + e + 1, :]
                        src = bass.AP(src.tensor, src.offset, [[0, HALF], [2 * N, n], [1, N]])
                        sp.dma_start(x0_rep[e * HALF:(e + 1) * HALF, bass.ds(half * T1 + QT * q, n), :],
                                     src).then_inc(rep_loaded[q], 16)

            sp.dma_start(ids_sb[:, :], ids).then_inc(ids_loaded, 16)
            sp.dma_start(base_sb[:, :], base).then_inc(ids_loaded, 16)
            sp.dma_start(w0a_sb, w0a).then_inc(w0_loaded, 16)
            sp.dma_start(w0b_sb, w0b).then_inc(w0_loaded, 16)
            for c in range(2):
                sp.wait_ge(x0_written, 16 * WRITES * (c + 1))
                if c:
                    sp.wait_ge(made, N0)
                load_layer0(c)
                if c:
                    for q in range(4):
                        sp.wait_ge(rep_loaded[q], 32 * c)
                load_replicated(c, c)
            with sp.Fori(1, C // 2) as pair:
                for half in range(2):
                    c = pair * 2 + half
                    for q in range(4):
                        sp.wait_ge(rep_loaded[q], 32 * c)
                    sp.wait_ge(x0_written, 16 * WRITES * (c + 1))
                    sp.wait_ge(made, groups_done(c - 2, N1 + N0 - 1))
                    load_layer0(c)
                    sp.wait_ge(made, groups_done(c - 2, PER_BODY - 1))
                    load_replicated(c, half)
            sp.wait_ge(y_ready, 1)
            sp.dma_start(out.rearrange("b a -> a b"), y_sb).then_inc(stored, 16)
            sp.wait_ge(stored, 16)

        @block.gpsimd
        def _(pool):
            pool.wait_ge(ids_loaded, 32)
            def gather(c, first=False):
                if not first:
                    pool.wait_ge(gather_done, 16 * GB * c)
                    pool.wait_ge(x0_written, 16 * WRITES * c)
                nc.gpsimd.tensor_tensor(rows_sb[:, :], ids_sb[:, bass.ds(c * GB, GB)],
                                        base_sb[:, 0:1].broadcast_to([GP, GB]), ALU.add).then_inc(rows_made, 1)
                pool.wait_ge(rows_made, c + 1)
                nc.gpsimd.tensor_tensor(fence[:, :], base_sb[0:1, :], base_sb[0:1, :], ALU.add)
                for j in range(GB):
                    pool.indirect_dma_start(out=gathered[:, j * D:(j + 1) * D], out_offset=None, in_=tables,
                                            in_offset=bass.IndirectOffsetOnAxis(ap=rows_sb[:, j:j + 1], axis=0)) \
                        .then_inc(gather_done, 16)
                pool.wait_ge(gather_done, 16 * GB * (c + 1))
                for g in range(GR):
                    skip = max(0, (G0[g - 1] + GB if g else 0) - G0[g])
                    cols = slice((G0[g] + skip) * D, (G0[g] + GB) * D)
                    pool.dma_start(x0_rows[bass.ds(c, 1), 0:F, cols].rearrange("a k n -> (a k) n"),
                                   gathered[g * F:(g + 1) * F, skip * D:GB * D]).then_inc(x0_written, 16)
                for g in range(GR):
                    skip = max(0, (G0[g - 1] + GB if g else 0) - G0[g])
                    cols = slice((G0[g] + skip) * D, (G0[g] + GB) * D)
                    pool.dma_start(x0_rows[bass.ds(c, 1), F:ROWS, cols].rearrange("a k n -> (a k) n"),
                                   gathered[g * F:g * F + ROWS - F, skip * D:GB * D]).then_inc(x0_written, 16)

            gather(0, first=True)
            with pool.Fori(1, C) as c:
                gather(c)

        @block.vector
        def _(dve):
            def multiply(c, group):
                layer, t, n, p, position = group
                slot = position % RING
                if layer == 0:
                    rep, row = x0_shifted[0:p, t:t + n, :], x0_same[0:p, :]
                else:
                    at = c % 2 * T1 + t if isinstance(c, int) else (c % 2) * T1 + t
                    rep, row = x0_rep[0:p, bass.ds(at, n), :], xk[layer - 1][0:p, :]
                nc.vector.tensor_tensor(products[0:p, slot:slot + n, :], rep,
                                        row.unsqueeze(1).broadcast_to([p, n, N]), ALU.mult).then_inc(made, 1)

            def logits01(c):
                dve.wait_ge(direct1_ready, c + 1)
                nc.vector.tensor_reduce(logit01[:, bass.ds(c * BC, BC)],
                                        direct01[:, :].rearrange("s (b d) -> s b d", d=D),
                                        axis=AX.X, op=ALU.add).then_inc(logit01_ready, 1)

            def logits2(c):
                dve.wait_ge(direct2_ready, c + 1)
                nc.vector.tensor_reduce(logit2[:, bass.ds(c * BC, BC)],
                                        direct2[:, :].rearrange("s (b d) -> s b d", d=D),
                                        axis=AX.X, op=ALU.add).then_inc(logit2_ready, 1)

            def body(c, first=False, last=False):
                for index, group in enumerate(BODY):
                    layer, t = group[0], group[1]
                    if layer == 0 and last:
                        continue
                    if not (first and group[4] < N0):
                        dve.wait_ge(used, slot_free(c, group))
                    if layer == 1:
                        if t == 0:
                            dve.wait_ge(xk0_ready, c + 1)
                        for q in {t // QT, (t + group[2] - 1) // QT}:
                            dve.wait_ge(rep_loaded[q], 32 * (c + 1))
                    if layer == 0 and t == 0:
                        dve.wait_ge(l0_loaded, 16 * L0_LOADS * (c + 2))
                    if layer == 2 and t == 0:
                        dve.wait_ge(xk1_ready, c + 1)
                    multiply(c, group)
                    if index == 3 and not first:
                        logits2(c - 1)
                    if index == N1 + N0 + 2:
                        logits01(c)

            dve.wait_ge(w0_loaded, 32)
            nc.vector.tensor_tensor(w0_sb[:, :, :], w0a_sb, w0b_sb, ALU.add).then_inc(w0_added, 1)
            dve.wait_ge(w0_added, 1)
            nc.vector.tensor_copy(w0_sb[0:F, 0, :], w0a_sb[0:F, 0, :]).then_inc(w0_folded, 1)
            dve.wait_ge(w0_folded, 1)
            dve.wait_ge(l0_loaded, 16 * L0_LOADS)
            for group in L0_GROUPS:
                multiply(0, group)
            body(0, first=True)
            with dve.Fori(1, C - 1) as c:
                body(c)
            body(C - 1, last=True)
            logits2(C - 1)

        @block.tensor
        def _(pe):
            weight = [w0_sb, w1_sb, w2_sb]
            tiles = [T0, T1, T1]

            def contract(c, index, group):
                layer, t, n, p, position = group
                pe.wait_ge(made, groups_done(c, index))
                for i in range(n):
                    mm = nc.tensor.matmul(z[layer][:, :], weight[layer][0:p, t + i, :],
                                          products[0:p, position % RING + i, :],
                                          start=(t + i == 0), stop=(t + i == tiles[layer] - 1))
                mm.then_inc(used, 1)

            def body(c, first=False, last=False):
                for index, group in enumerate(BODY):
                    layer, t = group[0], group[1]
                    if layer == 0 and last:
                        continue
                    if t == 0 and layer == 0:
                        pe.wait_ge(direct0_ready, c + 1)
                    if t == 0 and layer == 1:
                        if first:
                            pe.wait_ge(w1_loaded, 32)
                        else:
                            pe.wait_ge(direct1_ready, c)
                    if t == 0 and layer == 2:
                        if first:
                            pe.wait_ge(w2_loaded, 32)
                        else:
                            pe.wait_ge(direct2_ready, c)
                    if last and layer == 2:
                        index -= N0
                    contract(c, index, group)

            pe.wait_ge(w0_folded, 1)
            for index, group in enumerate(L0_GROUPS):
                contract(0, index - N0, group)
            body(0, first=True)
            with pe.Fori(1, C - 1) as c:
                body(c)
            body(C - 1, last=True)

            pe.wait_ge(top_loaded, 16 * 7)
            pe.wait_ge(logit01_ready, C)
            for m in range(H1 // 128):
                cols = slice(m * 128, (m + 1) * 128)
                nc.tensor.matmul(z_hidden1[m][:, :], wt1d_sb[:, cols], dense_sb[:, :], start=True, stop=False)
                nc.tensor.matmul(z_hidden1[m][:, :], wt1_sb[:, 0, cols], logit01[:, :], start=False, stop=False)
            pe.wait_ge(logit2_ready, C)
            for m in range(H1 // 128):
                cols = slice(m * 128, (m + 1) * 128)
                nc.tensor.matmul(z_hidden1[m][:, :], wt1_sb[:, 1, cols], logit2[:, :],
                                 start=False, stop=True).then_inc(hidden1_done, 1)
            for k in range(H1 // 128):
                pe.wait_ge(hidden1_ready, k + 1)
                for m in range(H2 // 128):
                    mm = nc.tensor.matmul(z_hidden2[m][:, :], wt2_sb[:, k, m * 128:(m + 1) * 128], hidden1[:, k, :],
                                          start=(k == 0), stop=(k == H1 // 128 - 1))
                    if k == H1 // 128 - 1:
                        mm.then_inc(hidden2_done, 1)
            for k in range(H2 // 128):
                pe.wait_ge(hidden2_ready, k + 1)
                mm = nc.tensor.matmul(z_y[0:1, :], wt3_sb[:, k:k + 1], hidden2[:, k, :],
                                      start=(k == 0), stop=(k == H2 // 128 - 1))
            mm.then_inc(y_done, 1)

        @block.scalar
        def _(act):
            act.dma_start(b0_sb[:, :], b0).then_inc(biases_loaded, 16)
            act.dma_start(bx0_sb[:, :], bx0).then_inc(biases_loaded, 16)
            act.dma_start(b1_sb[:, :], b1).then_inc(biases_loaded, 16)
            act.dma_start(bx1_sb[:, :], bx1).then_inc(biases_loaded, 16)
            act.dma_start(b2_sb[:, :], b2).then_inc(biases_loaded, 16)
            for w_sb, w, loaded in ((w1_sb, w1, w1_loaded), (w2_sb, w2, w2_loaded)):
                full = (T1 - 1) * S
                rows = w.rearrange("h k s -> (h k) s")
                act.dma_start(w_sb[:, 0:T1 - 1, :], rows[0:full, :].rearrange("(t p) s -> p t s", p=S)) \
                    .then_inc(loaded, 16)
                act.dma_start(w_sb[0:HALF, T1 - 1, :], rows[full:full + HALF, :]).then_inc(loaded, 16)
            act.dma_start(dense_sb[:, :], dense).then_inc(top_loaded, 16)
            act.dma_start(wt1_sb[:, :, :], wt1[0:256, :].rearrange("(t p) m -> p t m", p=128)).then_inc(top_loaded, 16)
            act.dma_start(wt1d_sb[:, :], wt1[256:256 + DENSE, :]).then_inc(top_loaded, 16)
            act.dma_start(wt2_sb[:, :, :], wt2.rearrange("(t p) m -> p t m", p=128)).then_inc(top_loaded, 16)
            act.dma_start(wt3_sb[:, :], wt3).then_inc(top_loaded, 16)
            act.dma_start(bt1_sb[:, :], bt1).then_inc(top_loaded, 16)
            act.dma_start(bt2_sb[:, :], bt2).then_inc(top_loaded, 16)

            def relu(out, in_, bias):
                return nc.scalar.activation(out, in_, RELU, bias=bias)

            def after_layer0(c, done, wait_logits):
                act.wait_ge(used, done)
                relu(xk[0][HALF:S, :], z[0][HALF:S, :], bx0_sb[HALF:S, :])
                relu(xk[0][0:HALF, :], z[0][HALF:S, :], bx0_sb[HALF:S, :]).then_inc(xk0_ready, 1)
                if wait_logits:
                    act.wait_ge(logit01_ready, c)
                relu(direct01[0:HALF, :], z[0][0:HALF, :], b0_sb[0:HALF, :]).then_inc(direct0_ready, 1)

            def body(c, first=False, last=False):
                act.wait_ge(used, groups_done(c, N1 - 1))
                relu(xk[1][0:HALF, :], z[1][0:HALF, :], bx1_sb[0:HALF, :])
                relu(xk[1][HALF:S, :], z[1][0:HALF, :], bx1_sb[0:HALF, :]).then_inc(xk1_ready, 1)
                relu(direct01[HALF:S, :], z[1][HALF:S, :], b1_sb[HALF:S, :]).then_inc(direct1_ready, 1)
                if not last:
                    after_layer0(c + 1, groups_done(c, N1 + N0 - 1), True)
                act.wait_ge(used, groups_done(c, PER_BODY - 1) - (N0 if last else 0))
                if not first:
                    act.wait_ge(logit2_ready, c)
                relu(direct2[:, :], z[2][:, :], b2_sb[:, :]).then_inc(direct2_ready, 1)

            act.wait_ge(biases_loaded, 16 * 5)
            after_layer0(0, N0, False)
            body(0, first=True)
            with act.Fori(1, C - 1) as c:
                body(c)
            body(C - 1, last=True)

            act.wait_ge(top_loaded, 16 * 7)
            for m in range(H1 // 128):
                act.wait_ge(hidden1_done, m + 1)
                relu(hidden1[:, m, :], z_hidden1[m][:, :], bt1_sb[:, m:m + 1]).then_inc(hidden1_ready, 1)
            for m in range(H2 // 128):
                act.wait_ge(hidden2_done, m + 1)
                relu(hidden2[:, m, :], z_hidden2[m][:, :], bt2_sb[:, m:m + 1]).then_inc(hidden2_ready, 1)
            act.wait_ge(y_done, 1)
            nc.scalar.activation(y_sb, z_y[0:1, :], ACT.Copy).then_inc(y_ready, 1)


def kernel(**inputs):
    import numpy as _np
    import concourse.bacc as _bacc
    from concourse import mybir as _mybir
    from concourse.bass_utils import run_bass_kernel_spmd as _run

    a = {k: _np.asarray(v) for k, v in inputs.items()}
    batch = (_np.arange(C)[None, :, None] * BC + _np.asarray(G0)[:, None, None] + _np.arange(GB)[None, None, :])
    ids = a["ids"][batch]
    ids = ids.transpose(0, 3, 1, 2).reshape(GP, C * GB)
    starts = _np.concatenate([[0], _np.cumsum(SIZES)[:-1]]).astype(_np.int32)
    base = _np.tile(starts, GR).reshape(GP, 1)
    tables = _np.concatenate([a[f"tbl_{f}"] for f in range(F)], axis=0)
    shift = _np.arange(T0)[None, None, :] * GR + _np.arange(GR)[:, None, None]
    k = _np.broadcast_to(_np.arange(F)[None, :, None], (GR, F, T0))
    other = (k + shift) % F
    order = _np.concatenate([_np.arange(HALF, S), _np.arange(HALF)])
    w0 = a["L0_rec_w0"][:, :, order]
    b0, b1 = a["L0_rec_b0"][order], a["L0_rec_b1"]
    arrays = {
        "ids": ids, "base": base, "tables": tables, "dense": a["dense_ctx"].T,
        "w0a": w0[k, other].reshape(GP, T0, S), "w0b": w0[other, k].reshape(GP, T0, S),
        "b0": b0.reshape(S, 1), "bx0": _np.tile(b0[HALF:], 2).reshape(S, 1),
        "w1": a["L0_rec_w1"], "b1": b1.reshape(S, 1), "bx1": _np.tile(b1[:HALF], 2).reshape(S, 1),
        "w2": a["L0_rec_w2"], "b2": a["L0_rec_b2"].reshape(S, 1),
        "wt1": a["W_top1"], "bt1": a["b_top1"].reshape(H1 // 128, 128).T,
        "wt2": a["W_top2"], "bt2": a["b_top2"].reshape(H2 // 128, 128).T,
        "wt3": a["W_top3"].reshape(H2 // 128, 128).T,
    }
    nc = _bacc.Bacc("TRN2", target_bir_lowering=False, num_devices=1)
    sent, args = {}, []
    for name, v in arrays.items():
        v = _np.ascontiguousarray(v)
        sent[f"in_{name}"] = v
        args.append(nc.dram_tensor(f"in_{name}", v.shape, _mybir.dt.from_np(v.dtype), kind="ExternalInput").ap())
    args.append(nc.dram_tensor("out_y", (B, 1), _mybir.dt.float32, kind="ExternalOutput").ap())
    dlrm_cin_kernel(nc, *args)
    return _run(nc, [sent], core_ids=[0]).results[0]["out_y"]
```

```python
import numpy as np
import concourse.bass as bass
from concourse import mybir
from contextlib import ExitStack

B, F, D = 512, 39, 16
SIZES = [1250, 1000, 125000, 1250, 1250, 125000, 125000, 125000, 125000, 1250, 1250, 12500, 12500,
         1000, 1000, 12500, 1250, 1250, 12500, 12500, 12500, 1250, 12500, 125000, 125000, 1250,
         125000, 1250, 12500, 1000, 125000, 125000, 12500, 1000, 125000, 1000, 1250, 1250, 12500]
S, HALF = 128, 64
BC = 32
N = BC * D
C = B // BC
GR, GB = 3, 11
G0 = [0, GB, BC - GB]
GP = GR * F
SH = (F + 1) // 2
T0 = -(-SH // GR)
ROWS = F + SH - 1
T1 = -(-F // 2)
QT = T1 // 4
DENSE = 16
H1, H2 = 512, 256

WHOLE, LOW_DVE, LOW_POOL = "whole", "low part by VectorE", "low part by GpSimd"
LETTER = {"w": WHOLE, "d": LOW_DVE, "p": LOW_POOL}
KINDS = {1: "wdwpwppddw", 0: "dwww", 2: "wwwwpwpdpw"}


def groups_of(layer, tiles, partitions):
    found, t = [], 0
    for letter in KINDS[layer]:
        n = min(2, tiles - t)
        found.append((layer, t, n, partitions[t:t + n], LETTER[letter]))
        t += n
    assert t == tiles
    return found


L1_GROUPS = groups_of(1, T1, [S] * (T1 - 1) + [HALF])
L0_GROUPS = groups_of(0, T0, [GP] * (T0 - 1) + [(SH - GR * (T0 - 1)) * F])
L2_GROUPS = groups_of(2, T1, [S] * (T1 - 1) + [HALF])
BODY = L1_GROUPS + L0_GROUPS + L2_GROUPS
N1, N0 = len(L1_GROUPS), len(L0_GROUPS)
LAYER0 = range(N1, N1 + N0)
SPLIT = [i for i, g in enumerate(BODY) if g[4] != WHOLE]

RING = 8
PART_RING = 3
TURN = -(-len(BODY) // RING) * RING
PART_TURN = -(-len(SPLIT) // PART_RING) * PART_RING
WHOLES = [i for i, g in enumerate(BODY) if g[4] == WHOLE]
WEIGHT_ORDER = [*LAYER0, *range(N1), *range(N1 + N0, len(BODY))]
GATHERS_BY = [0,0,11,11,11,11]
LOW_LAG = 1

COUNTED = {
    "all": lambda g: True,
    "split": lambda g: g[4] != WHOLE,
    LOW_DVE: lambda g: g[4] == LOW_DVE,
    LOW_POOL: lambda g: g[4] == LOW_POOL,
}


def count(what, c, index):
    counts = COUNTED[what]
    in_layer0 = sum(counts(BODY[i]) for i in LAYER0)
    here = sum(counts(g) for g in BODY[:index + 1])
    if isinstance(c, int) and c == -1:
        return here - sum(counts(g) for g in L1_GROUPS)
    if isinstance(c, int) and c == C - 1 and index >= N1 + N0:
        here -= in_layer0
    return c * sum(counts(g) for g in BODY) + (in_layer0 + here)


def before_in_slot(c, position, ring, turn, members):
    back = 0
    while True:
        position -= ring
        if position < 0:
            position, back = position + turn, back + 1
        if position >= len(members):
            continue
        index = members[position]
        if isinstance(c, int):
            if c - back < -1:
                return None
            if c - back == -1 and index not in LAYER0:
                continue
            if c - back == C - 1 and index in LAYER0:
                continue
        return c - back, index


def dlrm_cin_kernel(nc, ids, base, tables, dense, w0a, w0b, b0, bx0, w1, b1, bx1, w2, b2,
                    wt1, bt1, wt2, bt2, wt3, out):
    fp32, fp32r, i32 = mybir.dt.float32, mybir.dt.float32r, mybir.dt.int32
    ALU, ACT, AX = mybir.AluOpType, mybir.ActivationFunctionType, mybir.AxisListType
    RELU = ACT.Relu

    ctx = ExitStack()
    with ctx:
        def sb(name, shape, dt=fp32):
            return ctx.enter_context(nc.sbuf_tensor(name, shape, dt))

        def bank(name):
            return ctx.enter_context(nc.psum_tensor(name, [128, N], fp32))

        def sem(name):
            return ctx.enter_context(nc.semaphore(name))

        x0_rows = nc.dram_tensor("x0_rows", [C, ROWS, N], fp32, kind="Internal")

        ids_sb = sb("ids_sb", [GP, C * GB], i32)
        base_sb = sb("base_sb", [GP, 1], i32)
        rows_sb = sb("rows_sb", [GP, GB], i32)
        fence = sb("fence", [1, 1], i32)
        gathered = sb("gathered", [GP, GB * D])
        x0_same = sb("x0_same", [GP, N])
        x0_shifted = sb("x0_shifted", [GP, T0, N])
        x0_rep = sb("x0_rep", [128, 2 * T1, N])
        products = sb("products", [128, RING, 2, N])
        high = sb("high", [128, PART_RING, 2, N], fp32r)
        low = sb("low", [128, PART_RING, 2, N], fp32r)
        w_whole = sb("w_whole", [128, len(BODY) - len(SPLIT), 2, S])
        w_high = sb("w_high", [128, len(SPLIT), 2, S], fp32r)
        w_low = sb("w_low", [128, len(SPLIT), 2, S], fp32r)
        b0_sb, bx0_sb = sb("b0_sb", [128, 1]), sb("bx0_sb", [128, 1])
        b1_sb, bx1_sb = sb("b1_sb", [128, 1]), sb("bx1_sb", [128, 1])
        b2_sb = sb("b2_sb", [128, 1])
        direct01 = sb("direct01", [128, N])
        direct2 = sb("direct2", [128, N])
        logit01 = sb("logit01", [128, B])
        logit2 = sb("logit2", [128, B])
        bt1_sb = sb("bt1_sb", [128, H1 // 128])
        bt2_sb = sb("bt2_sb", [128, H2 // 128])
        def staged(first, p, tiles):
            flat = x0_rep[0:p, T1:2 * T1, :].rearrange("p t n -> p (t n)")
            return flat[:, first * S:(first + tiles) * S].rearrange("p (t s) -> p t s", s=S)

        w0a_sb, w0b_sb, w0_sb = staged(0, GP, T0), staged(T0, GP, T0), staged(2 * T0, GP, T0)
        w1_sb, w2_sb = staged(3 * T0, 128, T1), staged(3 * T0 + T1, 128, T1)
        w_sb = [w0_sb, w1_sb, w2_sb]

        wt1_sb = x0_rep[:, 0:2, :]
        wt1d_sb = x0_rep[0:DENSE, 2, :]
        dense_sb = x0_rep[0:DENSE, 3, :]
        wt2_sb = x0_rep[:, 4:4 + H1 * H2 // (128 * N), :].rearrange("p a n -> p (a n)") \
            .rearrange("p (t m) -> p t m", m=H2)
        wt3_sb = x0_rep[:, 4 + H1 * H2 // (128 * N), 0:H2 // 128]
        hidden1 = products[:, 0:2, :, :].rearrange("p a b n -> p (a b) n")
        hidden2 = products[:, 2, :, :]
        y_sb = products[0:1, 3, 0, :]

        z = [bank("z0"), bank("z1"), bank("z2")]
        xk = [bank("xk0"), bank("xk1")]
        spare = [bank("spare0"), bank("spare1"), bank("spare2")]
        z_hidden1 = [spare[0], spare[1], spare[2], z[0]]
        z_hidden2 = [z[1], xk[0]]
        z_y = xk[1]

        ids_loaded = sem("ids_loaded")
        rows_made = sem("rows_made")
        gather_done = sem("gather_done")
        x0_written = sem("x0_written")
        w0_loaded = sem("w0_loaded")
        w0_added = sem("w0_added")
        w0_folded = sem("w0_folded")
        w1_loaded = sem("w1_loaded")
        w2_loaded = sem("w2_loaded")
        w_rounded = sem("w_rounded")
        w_copied = sem("w_copied")
        biases_loaded = sem("biases_loaded")
        top_loaded = sem("top_loaded")
        l0_loaded = sem("l0_loaded")
        rep_loaded = [sem(f"rep_loaded{q}") for q in range(4)]
        made = sem("made")
        rounded = sem("rounded")
        low_by = {LOW_DVE: sem("low_by_dve"), LOW_POOL: sem("low_by_pool")}
        used = sem("used")
        xk0_ready, xk1_ready = sem("xk0_ready"), sem("xk1_ready")
        direct0_ready, direct1_ready = sem("direct0_ready"), sem("direct1_ready")
        direct2_ready = sem("direct2_ready")
        logit01_ready, logit2_ready = sem("logit01_ready"), sem("logit2_ready")
        hidden1_done, hidden1_ready = sem("hidden1_done"), sem("hidden1_ready")
        hidden2_done, hidden2_ready = sem("hidden2_done"), sem("hidden2_ready")
        y_done, y_ready = sem("y_done"), sem("y_ready")
        stored = sem("stored")

        def write_x0(engine, c):
            for first, last in ((0, F), (F, ROWS)):
                for g in range(GR):
                    skip = max(0, (G0[g - 1] + GB if g else 0) - G0[g])
                    cols = slice((G0[g] + skip) * D, (G0[g] + GB) * D)
                    engine.dma_start(x0_rows[bass.ds(c, 1), first:last, cols].rearrange("a k n -> (a k) n"),
                                 gathered[g * F:g * F + last - first, skip * D:GB * D]).then_inc(x0_written, 16)

        def part_slot(index):
            return SPLIT.index(index) % PART_RING

        def wait_slot(engine, c, index):
            before = before_in_slot(c, index, RING, TURN, range(len(BODY)))
            if before:
                kind = BODY[before[1]][4]
                engine.wait_ge(used if kind == WHOLE else low_by[kind],
                               count("all" if kind == WHOLE else kind, *before))

        def wait_part_slot(engine, c, index):
            before = before_in_slot(c, SPLIT.index(index), PART_RING, PART_TURN, SPLIT)
            if before:
                engine.wait_ge(used, count("all", *before))

        def low_part(engine, ops, c, index):
            _, _, n, (p, *_), kind = BODY[index]
            wait_part_slot(engine, c, index)
            engine.wait_ge(rounded, count("split", c, index))
            slot = part_slot(index)
            ops.tensor_tensor(low[0:p, slot, 0:n, :], products[0:p, index % RING, 0:n, :],
                              high[0:p, slot, 0:n, :].bitcast(fp32), ALU.subtract).then_inc(low_by[kind], 1)

        block = ctx.enter_context(nc.Block())
        WRITES = 2 * GR
        L0_LOADS = 2 * GR

        @block.sync
        def _(sp):
            def load_layer0(c):
                for r in range(GR):
                    n = T0 if GR * (T0 - 1) + r < SH else T0 - 1
                    sp.dma_start(x0_same[r * F:(r + 1) * F, :],
                                 x0_rows[bass.ds(c, 1), 0:F, :].rearrange("a k n -> (a k) n")).then_inc(l0_loaded, 16)
                    src = x0_rows[bass.ds(c, 1), r:r + F, :].rearrange("a k n -> (a k) n").unsqueeze(1)
                    src = bass.AP(src.tensor, src.offset, [[N, F], [GR * N, n], [1, N]])
                    sp.dma_start(x0_shifted[r * F:(r + 1) * F, 0:n, :], src).then_inc(l0_loaded, 16)

            def load_replicated(c, half):
                for q in range(4):
                    for e in range(2):
                        src = x0_rows[bass.ds(c, 1), 2 * QT * q + e:2 * QT * q + e + 1, :]
                        src = bass.AP(src.tensor, src.offset, [[0, HALF], [2 * N, QT], [1, N]])
                        sp.dma_start(x0_rep[e * HALF:(e + 1) * HALF, bass.ds(half * T1 + QT * q, QT), :],
                                     src).then_inc(rep_loaded[q], 16)

            sp.dma_start(ids_sb[:, :], ids).then_inc(ids_loaded, 16)
            sp.dma_start(base_sb[:, :], base).then_inc(ids_loaded, 16)
            sp.dma_start(w0a_sb, w0a).then_inc(w0_loaded, 16)
            sp.dma_start(w0b_sb, w0b).then_inc(w0_loaded, 16)
            for c in range(2):
                sp.wait_ge(gather_done, 16 * GB * (c + 1))
                write_x0(sp, c)
                sp.wait_ge(x0_written, 16 * WRITES * (c + 1))
                if c:
                    sp.wait_ge(made, count("all", c - 2, N1 + N0 - 1))
                load_layer0(c)
                if c:
                    sp.wait_ge(w_copied, len(BODY))
                    for q in range(4):
                        sp.wait_ge(rep_loaded[q], 32 * c)
                load_replicated(c, c)
            with sp.Fori(1, C // 2) as pair:
                for half in range(2):
                    c = pair * 2 + half
                    for q in range(4):
                        sp.wait_ge(rep_loaded[q], 32 * c)
                    sp.wait_ge(x0_written, 16 * WRITES * (c + 1))
                    sp.wait_ge(made, count("all", c - 2, N1 + N0 - 1))
                    load_layer0(c)
                    sp.wait_ge(made, count("all", c - 2, len(BODY) - 1))
                    load_replicated(c, half)
            sp.wait_ge(made, count("all", C - 2, len(BODY) - 1))
            sp.dma_start(dense_sb, dense).then_inc(top_loaded, 16)
            sp.dma_start(wt1_sb, wt1[0:256, :].rearrange("(t p) m -> p t m", p=128)).then_inc(top_loaded, 16)
            sp.dma_start(wt1d_sb, wt1[256:256 + DENSE, :]).then_inc(top_loaded, 16)
            sp.dma_start(wt2_sb, wt2.rearrange("(t p) m -> p t m", p=128)).then_inc(top_loaded, 16)
            sp.dma_start(wt3_sb, wt3).then_inc(top_loaded, 16)
            sp.wait_ge(y_ready, 1)
            sp.dma_start(out.rearrange("b a -> a b"), y_sb).then_inc(stored, 16)
            sp.wait_ge(stored, 16)

        @block.gpsimd
        def _(pool):
            def make_rows(c, first=False):
                if not first:
                    pool.wait_ge(gather_done, 16 * GB * c)
                    pool.wait_ge(x0_written, 16 * WRITES * c)
                nc.gpsimd.tensor_tensor(rows_sb[:, :], ids_sb[:, bass.ds(c * GB, GB)],
                                        base_sb[:, 0:1].broadcast_to([GP, GB]), ALU.add).then_inc(rows_made, 1)

            def gather(j):
                pool.indirect_dma_start(out=gathered[:, j * D:(j + 1) * D], out_offset=None, in_=tables,
                                        in_offset=bass.IndirectOffsetOnAxis(ap=rows_sb[:, j:j + 1], axis=0)) \
                    .then_inc(gather_done, 16)

            def body(c, gathers=True):
                last = isinstance(c, int) and c == C - 1
                mine = [i for i, g in enumerate(BODY) if g[4] == LOW_POOL and not (last and i in LAYER0)]
                if gathers:
                    make_rows(c + 2)
                sent = 0
                for n, index in enumerate(mine):
                    if gathers and n == 0:
                        pool.wait_ge(rows_made, c + 3)
                    low_part(pool, nc.gpsimd, c, index)
                    if gathers:
                        upto = GATHERS_BY[n]
                        for j in range(sent, upto):
                            gather(j)
                        sent = upto

            pool.wait_ge(ids_loaded, 32)
            for c in range(2):
                make_rows(c, first=(c == 0))
                pool.wait_ge(rows_made, c + 1)
                for j in range(GB):
                    gather(j)
            for index in LAYER0:
                if BODY[index][4] == LOW_POOL:
                    low_part(pool, nc.gpsimd, -1, index)
            body(0)
            with pool.Fori(1, C - 2) as c:
                body(c)
            body(C - 2, gathers=False)
            body(C - 1, gathers=False)

        @block.vector
        def _(dve):
            def multiply(c, index):
                layer, t, n, (p, *_), _ = BODY[index]
                if layer == 0:
                    rep, row = x0_shifted[0:p, t:t + n, :], x0_same[0:p, :]
                else:
                    rep, row = x0_rep[0:p, bass.ds(c % 2 * T1 + t, n), :], xk[layer - 1][0:p, :]
                nc.vector.tensor_tensor(products[0:p, index % RING, 0:n, :], rep,
                                        row.unsqueeze(1).broadcast_to([p, n, N]), ALU.mult).then_inc(made, 1)

            def logits01(c):
                dve.wait_ge(direct1_ready, c + 1)
                nc.vector.tensor_reduce(logit01[:, bass.ds(c * BC, BC)],
                                        direct01[:, :].rearrange("s (b d) -> s b d", d=D),
                                        axis=AX.X, op=ALU.add).then_inc(logit01_ready, 1)

            def logits2(c):
                dve.wait_ge(direct2_ready, c + 1)
                nc.vector.tensor_reduce(logit2[:, bass.ds(c * BC, BC)],
                                        direct2[:, :].rearrange("s (b d) -> s b d", d=D),
                                        axis=AX.X, op=ALU.add).then_inc(logit2_ready, 1)

            def body(c, indices):
                late = []
                for index in indices:
                    layer, t, n, _, kind = BODY[index]
                    if layer == 1:
                        if t == 0:
                            dve.wait_ge(xk0_ready, c + 1)
                        for q in {t // QT, (t + n - 1) // QT}:
                            dve.wait_ge(rep_loaded[q], 32 * (c + 1))
                    if layer == 0 and t == 0:
                        dve.wait_ge(l0_loaded, 16 * L0_LOADS * (c + 2))
                    if layer == 2 and t == 0:
                        dve.wait_ge(xk1_ready, c + 1)
                    wait_slot(dve, c, index)
                    multiply(c, index)
                    if kind == LOW_DVE:
                        late.append(index)
                    while late and late[0] <= index - LOW_LAG:
                        low_part(dve, nc.vector, c, late.pop(0))
                    if index == 8 and not (isinstance(c, int) and c == 0):
                        logits2(c - 1)
                    if index == N1 + N0 + 4:
                        logits01(c)
                for index in late:
                    low_part(dve, nc.vector, c, index)

            everything = range(len(BODY))
            dve.wait_ge(w0_loaded, 32)
            nc.vector.tensor_tensor(w0_sb, w0a_sb, w0b_sb, ALU.add).then_inc(w0_added, 1)
            dve.wait_ge(w0_added, 1)
            nc.vector.tensor_copy(w0_sb[0:F, 0, :], w0a_sb[0:F, 0, :]).then_inc(w0_folded, 1)
            dve.wait_ge(w0_folded, 1)
            for n_taken, index in enumerate(WEIGHT_ORDER):
                layer, t, n, (p, *_), kind = BODY[index]
                if index == 0:
                    dve.wait_ge(w1_loaded, 48)
                if index == N1 + N0:
                    dve.wait_ge(w2_loaded, 48)
                if kind == WHOLE:
                    nc.vector.tensor_copy(w_whole[0:p, WHOLES.index(index), 0:n, :],
                                          w_sb[layer][0:p, t:t + n, :]).then_inc(w_copied, 1)
                else:
                    at = SPLIT.index(index)
                    dve.wait_ge(w_rounded, sum(BODY[i][4] != WHOLE for i in WEIGHT_ORDER[:n_taken + 1]))
                    nc.vector.tensor_tensor(w_low[0:p, at, 0:n, :], w_sb[layer][0:p, t:t + n, :],
                                            w_high[0:p, at, 0:n, :].bitcast(fp32),
                                            ALU.subtract).then_inc(w_copied, 1)
            body(-1, LAYER0)
            body(0, everything)
            with dve.Fori(1, C - 1) as c:
                body(c, everything)
            body(C - 1, [i for i in everything if i not in LAYER0])
            logits2(C - 1)

        @block.tensor
        def _(pe):
            tiles = [T0, T1, T1]

            def contract(c, index):
                layer, t, n, partitions, kind = BODY[index]
                slot, out = index % RING, z[layer][:, :]
                if kind == WHOLE:
                    at = WHOLES.index(index)
                    pe.wait_ge(made, count("all", c, index))
                    for i, p in enumerate(partitions):
                        mm = nc.tensor.matmul(out, w_whole[0:p, at, i, :], products[0:p, slot, i, :],
                                              start=(t + i == 0), stop=(t + i == tiles[layer] - 1))
                else:
                    at, part = SPLIT.index(index), part_slot(index)
                    pe.wait_ge(rounded, count("split", c, index))
                    for i, p in enumerate(partitions):
                        nc.tensor.matmul(out, w_high[0:p, at, i, :], high[0:p, part, i, :],
                                         start=(t + i == 0), stop=False)
                        nc.tensor.matmul(out, w_low[0:p, at, i, :], high[0:p, part, i, :], start=False, stop=False)
                    pe.wait_ge(low_by[kind], count(kind, c, index))
                    for i, p in enumerate(partitions):
                        mm = nc.tensor.matmul(out, w_high[0:p, at, i, :], low[0:p, part, i, :],
                                              start=False, stop=(t + i == tiles[layer] - 1))
                mm.then_inc(used, 1)

            def body(c, indices):
                first = isinstance(c, int) and c == 0
                for index in indices:
                    layer, t = BODY[index][:2]
                    if t == 0 and layer == 0 and not (isinstance(c, int) and c < 0):
                        pe.wait_ge(direct0_ready, c + 1)
                    if t == 0 and layer == 1 and not first:
                        pe.wait_ge(direct1_ready, c)
                    if t == 0 and layer == 2 and not first:
                        pe.wait_ge(direct2_ready, c)
                    contract(c, index)

            everything = range(len(BODY))
            pe.wait_ge(w_copied, len(BODY))
            body(-1, LAYER0)
            body(0, everything)
            with pe.Fori(1, C - 1) as c:
                body(c, everything)
            body(C - 1, [i for i in everything if i not in LAYER0])

            pe.wait_ge(top_loaded, 16 * 5)
            pe.wait_ge(logit01_ready, C)
            for m in range(H1 // 128):
                cols = slice(m * 128, (m + 1) * 128)
                nc.tensor.matmul(z_hidden1[m][:, :], wt1d_sb[:, cols], dense_sb, start=True, stop=False)
                nc.tensor.matmul(z_hidden1[m][:, :], wt1_sb[:, 0, cols], logit01[:, :], start=False, stop=False)
            pe.wait_ge(logit2_ready, C)
            for m in range(H1 // 128):
                cols = slice(m * 128, (m + 1) * 128)
                nc.tensor.matmul(z_hidden1[m][:, :], wt1_sb[:, 1, cols], logit2[:, :],
                                 start=False, stop=True).then_inc(hidden1_done, 1)
            for k in range(H1 // 128):
                pe.wait_ge(hidden1_ready, k + 1)
                for m in range(H2 // 128):
                    mm = nc.tensor.matmul(z_hidden2[m][:, :], wt2_sb[:, k, m * 128:(m + 1) * 128], hidden1[:, k, :],
                                          start=(k == 0), stop=(k == H1 // 128 - 1))
                    if k == H1 // 128 - 1:
                        mm.then_inc(hidden2_done, 1)
            for k in range(H2 // 128):
                pe.wait_ge(hidden2_ready, k + 1)
                mm = nc.tensor.matmul(z_y[0:1, :], wt3_sb[:, k:k + 1], hidden2[:, k, :],
                                      start=(k == 0), stop=(k == H2 // 128 - 1))
            mm.then_inc(y_done, 1)

        @block.scalar
        def _(act):
            act.dma_start(b0_sb[:, :], b0).then_inc(biases_loaded, 16)
            act.dma_start(bx0_sb[:, :], bx0).then_inc(biases_loaded, 16)
            act.dma_start(b1_sb[:, :], b1).then_inc(biases_loaded, 16)
            act.dma_start(bx1_sb[:, :], bx1).then_inc(biases_loaded, 16)
            act.dma_start(b2_sb[:, :], b2).then_inc(biases_loaded, 16)
            for staging, w, loaded in ((w1_sb, w1, w1_loaded), (w2_sb, w2, w2_loaded)):
                full = (T1 - 1) * S
                rows = w.rearrange("h k s -> (h k) s")
                act.dma_start(staging[:, 0:T1 - 1, :], rows[0:full, :].rearrange("(t p) s -> p t s", p=S)) \
                    .then_inc(loaded, 16)
                for e in range(2):
                    act.dma_start(staging[e * HALF:(e + 1) * HALF, T1 - 1, :],
                                  rows[full:full + HALF, :]).then_inc(loaded, 16)
            act.dma_start(bt1_sb[:, :], bt1).then_inc(biases_loaded, 16)
            act.dma_start(bt2_sb[:, :], bt2).then_inc(biases_loaded, 16)

            def relu(out, in_, bias):
                return nc.scalar.activation(out, in_, RELU, bias=bias)

            def round_high(c, index):
                _, _, n, (p, *_), _ = BODY[index]
                slot = part_slot(index)
                wait_part_slot(act, c, index)
                act.wait_ge(made, count("all", c, index))
                nc.scalar.activation(high[0:p, slot, 0:n, :], products[0:p, index % RING, 0:n, :],
                                     ACT.Copy).then_inc(rounded, 1)

            def after_layer0(c):
                act.wait_ge(used, count("all", c, N1 + N0 - 1))
                relu(xk[0][HALF:S, :], z[0][HALF:S, :], bx0_sb[HALF:S, :])
                relu(xk[0][0:HALF, :], z[0][HALF:S, :], bx0_sb[HALF:S, :]).then_inc(xk0_ready, 1)
                if not (isinstance(c, int) and c < 0):
                    act.wait_ge(logit01_ready, c + 1)
                relu(direct01[0:HALF, :], z[0][0:HALF, :], b0_sb[0:HALF, :]).then_inc(direct0_ready, 1)

            def after_layer1(c):
                act.wait_ge(used, count("all", c, N1 - 1))
                relu(xk[1][0:HALF, :], z[1][0:HALF, :], bx1_sb[0:HALF, :])
                relu(xk[1][HALF:S, :], z[1][0:HALF, :], bx1_sb[0:HALF, :]).then_inc(xk1_ready, 1)
                relu(direct01[HALF:S, :], z[1][HALF:S, :], b1_sb[HALF:S, :]).then_inc(direct1_ready, 1)

            def after_layer2(c, first=False):
                act.wait_ge(used, count("all", c, len(BODY) - 1))
                if not first:
                    act.wait_ge(logit2_ready, c)
                relu(direct2[:, :], z[2][:, :], b2_sb[:, :]).then_inc(direct2_ready, 1)

            def body(c):
                first, last = isinstance(c, int) and c == 0, isinstance(c, int) and c == C - 1
                gathers = not isinstance(c, int) or c < C - 2
                for index in range(len(BODY)):
                    if index == 23 and gathers:
                        act.wait_ge(gather_done, 16 * GB * (c + 3))
                        write_x0(act, c + 2)
                    if index == 5 and not first:
                        after_layer2(c - 1, first=isinstance(c, int) and c == 1)
                    if index == N1 + 2:
                        after_layer1(c)
                    if index == N1 + N0 + 4 and not last:
                        after_layer0(c)
                    if index in SPLIT and not (last and index in LAYER0):
                        round_high(c, index)

            for n_taken, index in enumerate(WEIGHT_ORDER):
                layer, t, n, (p, *_), kind = BODY[index]
                if index == N1:
                    act.wait_ge(w0_folded, 1)
                if index == 0:
                    act.wait_ge(w1_loaded, 48)
                if index == N1 + N0:
                    act.wait_ge(w2_loaded, 48)
                if kind != WHOLE:
                    nc.scalar.activation(w_high[0:p, SPLIT.index(index), 0:n, :],
                                         w_sb[layer][0:p, t:t + n, :], ACT.Copy).then_inc(w_rounded, 1)
            act.wait_ge(biases_loaded, 16 * 7)
            for index in LAYER0:
                if index in SPLIT:
                    round_high(-1, index)
            after_layer0(-1)
            body(0)
            body(1)
            with act.Fori(2, C - 2) as c:
                body(c)
            body(C - 2)
            body(C - 1)
            after_layer2(C - 1)

            for m in range(H1 // 128):
                act.wait_ge(hidden1_done, m + 1)
                relu(hidden1[:, m, :], z_hidden1[m][:, :], bt1_sb[:, m:m + 1]).then_inc(hidden1_ready, 1)
            for m in range(H2 // 128):
                act.wait_ge(hidden2_done, m + 1)
                relu(hidden2[:, m, :], z_hidden2[m][:, :], bt2_sb[:, m:m + 1]).then_inc(hidden2_ready, 1)
            act.wait_ge(y_done, 1)
            nc.scalar.activation(y_sb, z_y[0:1, :], ACT.Copy).then_inc(y_ready, 1)


def kernel(**inputs):
    import numpy as _np
    import concourse.bacc as _bacc
    from concourse import mybir as _mybir
    from concourse.bass_utils import run_bass_kernel_spmd as _run

    a = {k: _np.asarray(v) for k, v in inputs.items()}
    batch = (_np.arange(C)[None, :, None] * BC + _np.asarray(G0)[:, None, None] + _np.arange(GB)[None, None, :])
    ids = a["ids"][batch]
    ids = ids.transpose(0, 3, 1, 2).reshape(GP, C * GB)
    starts = _np.concatenate([[0], _np.cumsum(SIZES)[:-1]]).astype(_np.int32)
    base = _np.tile(starts, GR).reshape(GP, 1)
    tables = _np.concatenate([a[f"tbl_{f}"] for f in range(F)], axis=0)
    shift = _np.arange(T0)[None, None, :] * GR + _np.arange(GR)[:, None, None]
    k = _np.broadcast_to(_np.arange(F)[None, :, None], (GR, F, T0))
    other = (k + shift) % F
    order = _np.concatenate([_np.arange(HALF, S), _np.arange(HALF)])
    w0 = a["L0_rec_w0"][:, :, order]
    b0, b1 = a["L0_rec_b0"][order], a["L0_rec_b1"]
    arrays = {
        "ids": ids, "base": base, "tables": tables, "dense": a["dense_ctx"].T,
        "w0a": w0[k, other].reshape(GP, T0, S), "w0b": w0[other, k].reshape(GP, T0, S),
        "b0": b0.reshape(S, 1), "bx0": _np.tile(b0[HALF:], 2).reshape(S, 1),
        "w1": a["L0_rec_w1"], "b1": b1.reshape(S, 1), "bx1": _np.tile(b1[:HALF], 2).reshape(S, 1),
        "w2": a["L0_rec_w2"], "b2": a["L0_rec_b2"].reshape(S, 1),
        "wt1": a["W_top1"], "bt1": a["b_top1"].reshape(H1 // 128, 128).T,
        "wt2": a["W_top2"], "bt2": a["b_top2"].reshape(H2 // 128, 128).T,
        "wt3": a["W_top3"].reshape(H2 // 128, 128).T,
    }
    nc = _bacc.Bacc("TRN2", target_bir_lowering=False, num_devices=1)
    sent, args = {}, []
    for name, v in arrays.items():
        v = _np.ascontiguousarray(v)
        sent[f"in_{name}"] = v
        args.append(nc.dram_tensor(f"in_{name}", v.shape, _mybir.dt.from_np(v.dtype), kind="ExternalInput").ap())
    args.append(nc.dram_tensor("out_y", (B, 1), _mybir.dt.float32, kind="ExternalOutput").ap())
    dlrm_cin_kernel(nc, *args)
    return _run(nc, [sent], core_ids=[0]).results[0]["out_y"]
```

```python
import numpy as np
import concourse.bass as bass
from concourse import mybir
from contextlib import ExitStack

B, F, D = 512, 39, 16
SIZES = [1250, 1000, 125000, 1250, 1250, 125000, 125000, 125000, 125000, 1250, 1250, 12500, 12500,
         1000, 1000, 12500, 1250, 1250, 12500, 12500, 12500, 1250, 12500, 125000, 125000, 1250,
         125000, 1250, 12500, 1000, 125000, 125000, 12500, 1000, 125000, 1000, 1250, 1250, 12500]
S, HALF = 128, 64
BC = 32
N = BC * D
C = B // BC
GR, GB = 3, 11
PITCH = GR * GB * D
GP = GR * F
assert GR * GB >= BC
SH = (F + 1) // 2
T0 = -(-SH // GR)
ROWS = 2 * F
assert GR * T0 - SH in (0, 1) and T0 * GR - 1 + F <= ROWS
T1 = -(-F // 2)
QT = T1 // 4
DENSE = 16
H1, H2 = 512, 256

WHOLE, LOW_DVE, LOW_POOL = "whole", "low part by VectorE", "low part by GpSimd"
STACKED = "whole, its second tile split and stacked"
LETTER = {"w": WHOLE, "d": LOW_DVE, "p": LOW_POOL, "h": STACKED}
KINDS = {1: "wpwpwppddh", 0: "wdww", 2: "wpwpwwpdph"}


def groups_of(layer, tiles, partitions):
    found, t = [], 0
    for letter in KINDS[layer]:
        n = min(2, tiles - t)
        found.append((layer, t, n, partitions[t:t + n], LETTER[letter]))
        t += n
    assert t == tiles
    return found


L1_GROUPS = groups_of(1, T1, [S] * (T1 - 1) + [HALF])
L0_GROUPS = groups_of(0, T0, [GP] * (T0 - 1) + [(SH - GR * (T0 - 1)) * F])
L2_GROUPS = groups_of(2, T1, [S] * (T1 - 1) + [HALF])
BODY = L1_GROUPS + L0_GROUPS + L2_GROUPS
N1, N0 = len(L1_GROUPS), len(L0_GROUPS)
LAYER0 = range(N1, N1 + N0)
SPLIT = [i for i, g in enumerate(BODY) if g[4] in (LOW_DVE, LOW_POOL)]
STACKS = [i for i, g in enumerate(BODY) if g[4] == STACKED]

RING = 8
PART_RING = 3
TURN = -(-len(BODY) // RING) * RING
PART_TURN = -(-len(SPLIT) // PART_RING) * PART_RING
WHOLES = [i for i, g in enumerate(BODY) if g[4] in (WHOLE, STACKED)]
WEIGHT_ORDER = [*LAYER0, *range(N1), *range(N1 + N0, len(BODY))]
GATHERS_BY = [0, 0, 0, 11, 11, 11, 11, 11]
FIRST_GATHERS = next(n for n, upto in enumerate(GATHERS_BY) if upto)
PAIRED = [0,2]
assert all(i % 2 == 0 and BODY[i][:1] == BODY[i + 1][:1] and BODY[i][3] == BODY[i + 1][3] for i in PAIRED)
LOW_LAG = 2

COUNTED = {
    "all": lambda g: True,
    "split": lambda g: g[4] in (LOW_DVE, LOW_POOL),
    "stacked": lambda g: g[4] == STACKED,
    LOW_DVE: lambda g: g[4] == LOW_DVE,
    LOW_POOL: lambda g: g[4] == LOW_POOL,
}


def count(what, c, index):
    counts = COUNTED[what]
    in_layer0 = sum(counts(BODY[i]) for i in LAYER0)
    here = sum(counts(g) for g in BODY[:index + 1])
    if isinstance(c, int) and c == -1:
        return here - sum(counts(g) for g in L1_GROUPS)
    if isinstance(c, int) and c == C - 1 and index >= N1 + N0:
        here -= in_layer0
    return c * sum(counts(g) for g in BODY) + (in_layer0 + here)


def before_in_slot(c, position, ring, turn, members):
    back = 0
    while True:
        position -= ring
        if position < 0:
            position, back = position + turn, back + 1
        if position >= len(members):
            continue
        index = members[position]
        if isinstance(c, int):
            if c - back < -1:
                return None
            if c - back == -1 and index not in LAYER0:
                continue
            if c - back == C - 1 and index in LAYER0:
                continue
        return c - back, index


def dlrm_cin_kernel(nc, ids, base, tables, dense, w0a, w0b, b0, bx0, w1, b1, bx1, w2, b2,
                    wt1, bt1, wt2, bt2, wt3, out):
    fp32, fp32r, i32 = mybir.dt.float32, mybir.dt.float32r, mybir.dt.int32
    ALU, ACT, AX = mybir.AluOpType, mybir.ActivationFunctionType, mybir.AxisListType
    RELU = ACT.Relu

    ctx = ExitStack()
    with ctx:
        def sb(name, shape, dt=fp32):
            return ctx.enter_context(nc.sbuf_tensor(name, shape, dt))

        def bank(name):
            return ctx.enter_context(nc.psum_tensor(name, [128, N], fp32))

        def sem(name):
            return ctx.enter_context(nc.semaphore(name))

        x0_rows = nc.dram_tensor("x0_rows", [C, ROWS, PITCH], fp32, kind="Internal")

        ids_sb = sb("ids_sb", [GP, C * GB], i32)
        base_sb = sb("base_sb", [GP, 1], i32)
        rows_sb = sb("rows_sb", [GP, GB], i32)
        gathered = sb("gathered", [GP, GB * D])
        x0_same = sb("x0_same", [GP, N])
        x0_shifted = sb("x0_shifted", [GP, T0, PITCH])
        x0_rep = sb("x0_rep", [128, 2 * T1, N])
        products = sb("products", [128, RING, 2, N])
        high = sb("high", [128, PART_RING, 2, N], fp32r)
        low = sb("low", [128, PART_RING, 2, N], fp32r)
        stacks = sb("stacks", [128, len(STACKS), N], fp32r)
        w_whole = sb("w_whole", [128, len(WHOLES), 2, S])
        w_stack_high = sb("w_stack_high", [128, len(STACKS), S], fp32r)
        w_stack_low = sb("w_stack_low", [HALF, len(STACKS), S], fp32r)
        w_high = sb("w_high", [128, len(SPLIT), 2, S], fp32r)
        w_low = sb("w_low", [128, len(SPLIT), 2, S], fp32r)
        b0_sb, bx0_sb = sb("b0_sb", [128, 1]), sb("bx0_sb", [128, 1])
        b1_sb, bx1_sb = sb("b1_sb", [128, 1]), sb("bx1_sb", [128, 1])
        b2_sb = sb("b2_sb", [128, 1])
        direct01 = sb("direct01", [128, N])
        direct2 = sb("direct2", [128, N])
        logit01 = sb("logit01", [128, B])
        logit2 = sb("logit2", [128, B])
        bt1_sb = sb("bt1_sb", [128, H1 // 128])
        bt2_sb = sb("bt2_sb", [128, H2 // 128])
        def staged(first, p, tiles):
            flat = x0_rep[0:p, T1:2 * T1, :].rearrange("p t n -> p (t n)")
            return flat[:, first * S:(first + tiles) * S].rearrange("p (t s) -> p t s", s=S)

        w0a_sb, w0b_sb, w0_sb = staged(0, GP, T0), staged(T0, GP, T0), staged(2 * T0, GP, T0)
        w1_sb, w2_sb = staged(3 * T0, 128, T1), staged(3 * T0 + T1, 128, T1)
        w_sb = [w0_sb, w1_sb, w2_sb]

        wt1_sb = x0_rep[:, 0:2, :]
        wt1d_sb = x0_rep[0:DENSE, 2, :]
        dense_sb = x0_rep[0:DENSE, 3, :]
        wt2_sb = x0_rep[:, 4:4 + H1 * H2 // (128 * N), :].rearrange("p a n -> p (a n)") \
            .rearrange("p (t m) -> p t m", m=H2)
        wt3_sb = x0_rep[:, 4 + H1 * H2 // (128 * N), 0:H2 // 128]
        early_dense = products[0:DENSE, RING - 1, 0, :]
        early_wt1d = products[0:DENSE, RING - 1, 1, :]
        assert all(i % RING != RING - 1 for i in LAYER0)
        hidden1 = products[:, 0:2, :, :].rearrange("p a b n -> p (a b) n")
        hidden2 = products[:, 2, :, :]
        y_sb = products[0:1, 3, 0, :]

        z = [bank("z0"), bank("z1"), bank("z2")]
        xk = [bank("xk0"), bank("xk1")]
        spare = [bank("spare0"), bank("spare1"), bank("spare2")]
        EARLY = len(spare)
        z_hidden1 = [spare[0], spare[1], spare[2], z[0]]
        z_hidden2 = [z[1], xk[0]]
        z_y = xk[1]

        ids_loaded = sem("ids_loaded")
        rows_made = sem("rows_made")
        gather_done = sem("gather_done")
        x0_written = sem("x0_written")
        w0_loaded = sem("w0_loaded")
        w0_added = sem("w0_added")
        w0_folded = sem("w0_folded")
        w1_loaded = sem("w1_loaded")
        w2_loaded = sem("w2_loaded")
        w_rounded = sem("w_rounded")
        w_copied = sem("w_copied")
        biases_loaded = sem("biases_loaded")
        early_loaded = sem("early_loaded")
        top_loaded = sem("top_loaded")
        same_loaded = sem("same_loaded")
        shifted_loaded = [sem(f"shifted_loaded{i}") for i in range(N0)]
        l0_loaded = sem("l0_loaded")
        rep_loaded = [sem(f"rep_loaded{q}") for q in range(4)]
        made = sem("made")
        rounded = sem("rounded")
        low_by = {LOW_DVE: sem("low_by_dve"), LOW_POOL: sem("low_by_pool")}
        stack_rounded, stack_low = sem("stack_rounded"), sem("stack_low")
        w_stack_rounded, w_stack_made = sem("w_stack_rounded"), sem("w_stack_made")
        used = sem("used")
        xk0_ready, xk1_ready = sem("xk0_ready"), sem("xk1_ready")
        direct0_ready, direct1_ready = sem("direct0_ready"), sem("direct1_ready")
        direct2_ready = sem("direct2_ready")
        logit01_ready, logit2_ready = sem("logit01_ready"), sem("logit2_ready")
        hidden1_done, hidden1_ready = sem("hidden1_done"), sem("hidden1_ready")
        hidden2_done, hidden2_ready = sem("hidden2_done"), sem("hidden2_ready")
        y_done, y_ready = sem("y_done"), sem("y_ready")
        stored = sem("stored")

        def write_x0(engine, c):
            for first in (0, F):
                dst = x0_rows[bass.ds(c, 1), first:first + F, :].rearrange("a k (g n) -> (a g) k n", g=GR)
                engine.dma_start(dst, gathered[:, :]).then_inc(x0_written, 16)

        def part_slot(index):
            return SPLIT.index(index) % PART_RING

        def wait_slot(engine, c, index):
            before = before_in_slot(c, index, RING, TURN, range(len(BODY)))
            if before:
                kind = BODY[before[1]][4]
                if kind in low_by:
                    engine.wait_ge(low_by[kind], count(kind, *before))
                else:
                    engine.wait_ge(used, count("all", *before))

        def wait_part_slot(engine, c, index):
            before = before_in_slot(c, SPLIT.index(index), PART_RING, PART_TURN, SPLIT)
            if before:
                engine.wait_ge(used, count("all", *before))

        def low_part(engine, ops, c, index):
            _, _, n, (p, *_), kind = BODY[index]
            wait_part_slot(engine, c, index)
            engine.wait_ge(rounded, count("split", c, index))
            slot = part_slot(index)
            ops.tensor_tensor(low[0:p, slot, 0:n, :], products[0:p, index % RING, 0:n, :],
                              high[0:p, slot, 0:n, :].bitcast(fp32), ALU.subtract).then_inc(low_by[kind], 1)

        block = ctx.enter_context(nc.Block())
        WRITES = 2
        L0_LOADS = 2

        @block.sync
        def _(sp):
            def load_same(c, loaded):
                src = x0_rows[bass.ds(c, 1), 0:1, 0:N]
                src = bass.AP(src.tensor, src.offset, [[0, GR], [PITCH, F], [1, N]])
                sp.dma_start(x0_same[:, :], src).then_inc(loaded, 16)

            def load_shifted(c, t, n, loaded):
                src = x0_rows[bass.ds(c, 1), t:t + 1, :]
                src = bass.AP(src.tensor, src.offset, [[T0 * PITCH, GR], [PITCH, F], [1, n * PITCH]])
                sp.dma_start(x0_shifted[:, t:t + n, :].rearrange("p t n -> p (t n)"), src).then_inc(loaded, 16)

            def load_layer0(c):
                load_same(c, l0_loaded)
                load_shifted(c, 0, T0, l0_loaded)

            def load_replicated(c, half, quarters=range(4)):
                for q in quarters:
                    for e in range(2):
                        src = x0_rows[bass.ds(c, 1), 2 * QT * q + e:2 * QT * q + e + 1, 0:N]
                        src = bass.AP(src.tensor, src.offset, [[0, HALF], [2 * PITCH, QT], [1, N]])
                        sp.dma_start(x0_rep[e * HALF:(e + 1) * HALF, bass.ds(half * T1 + QT * q, QT), :],
                                     src).then_inc(rep_loaded[q], 16)

            sp.dma_start(ids_sb[:, :], ids).then_inc(ids_loaded, 16)
            sp.dma_start(base_sb[:, :], base).then_inc(ids_loaded, 16)
            sp.dma_start(w0a_sb, w0a).then_inc(w0_loaded, 16)
            sp.dma_start(w0b_sb, w0b).then_inc(w0_loaded, 16)
            sp.wait_ge(gather_done, 16 * GB)
            write_x0(sp, 0)
            sp.wait_ge(x0_written, 16 * WRITES)
            load_same(0, same_loaded)
            for index in LAYER0:
                load_shifted(0, *BODY[index][1:3], shifted_loaded[index - N1])
            load_replicated(0, 0, range(2))
            sp.wait_ge(gather_done, 16 * GB * 2)
            write_x0(sp, 1)
            load_replicated(0, 0, range(2, 4))
            sp.wait_ge(x0_written, 16 * WRITES * 2)
            sp.wait_ge(made, count("all", -1, N1 + N0 - 1))
            load_layer0(1)
            sp.wait_ge(w_copied, len(BODY))
            sp.wait_ge(w_stack_made, len(STACKS))
            for q in range(4):
                sp.wait_ge(rep_loaded[q], 32)
            load_replicated(1, 1)
            with sp.Fori(1, C // 2) as pair:
                for half in range(2):
                    c = pair * 2 + half
                    for q in range(4):
                        sp.wait_ge(rep_loaded[q], 32 * c)
                    sp.wait_ge(x0_written, 16 * WRITES * (c + 1))
                    sp.wait_ge(made, count("all", c - 2, N1 + N0 - 1))
                    load_layer0(c)
                    sp.wait_ge(made, count("all", c - 2, len(BODY) - 1))
                    load_replicated(c, half)
            sp.wait_ge(made, count("all", C - 2, len(BODY) - 1))
            sp.dma_start(dense_sb, dense).then_inc(top_loaded, 16)
            sp.dma_start(wt1_sb, wt1[0:256, :].rearrange("(t p) m -> p t m", p=128)).then_inc(top_loaded, 16)
            sp.dma_start(wt1d_sb, wt1[256:256 + DENSE, :]).then_inc(top_loaded, 16)
            sp.dma_start(wt2_sb, wt2.rearrange("(t p) m -> p t m", p=128)).then_inc(top_loaded, 16)
            sp.dma_start(wt3_sb, wt3).then_inc(top_loaded, 16)
            sp.wait_ge(y_ready, 1)
            sp.dma_start(out.rearrange("b a -> a b"), y_sb).then_inc(stored, 16)
            sp.wait_ge(stored, 16)

        @block.gpsimd
        def _(pool):
            def make_rows(c, first=False):
                if not first:
                    pool.wait_ge(gather_done, 16 * GB * c)
                    pool.wait_ge(x0_written, 16 * WRITES * c)
                nc.gpsimd.tensor_tensor(rows_sb[:, :], ids_sb[:, bass.ds(c * GB, GB)],
                                        base_sb[:, 0:1].broadcast_to([GP, GB]), ALU.add).then_inc(rows_made, 1)

            def gather(j):
                pool.indirect_dma_start(out=gathered[:, j * D:(j + 1) * D], out_offset=None, in_=tables,
                                        in_offset=bass.IndirectOffsetOnAxis(ap=rows_sb[:, j:j + 1], axis=0)) \
                    .then_inc(gather_done, 16)

            def body(c, gathers=True):
                last = isinstance(c, int) and c == C - 1
                mine = [i for i, g in enumerate(BODY) if g[4] == LOW_POOL and not (last and i in LAYER0)]
                sent = 0
                for n, index in enumerate(mine):
                    if gathers and n == 0:
                        make_rows(c + 2)
                    if gathers and n == FIRST_GATHERS:
                        pool.wait_ge(rows_made, c + 3)
                    low_part(pool, nc.gpsimd, c, index)
                    if gathers:
                        upto = GATHERS_BY[n]
                        for j in range(sent, upto):
                            gather(j)
                        sent = upto

            pool.wait_ge(ids_loaded, 32)
            for c in range(2):
                make_rows(c, first=(c == 0))
                pool.wait_ge(rows_made, c + 1)
                for j in range(GB):
                    gather(j)
            for index in LAYER0:
                if BODY[index][4] == LOW_POOL:
                    low_part(pool, nc.gpsimd, -1, index)
            body(0)
            with pool.Fori(1, C - 2) as c:
                body(c)
            body(C - 2, gathers=False)
            body(C - 1, gathers=False)

        @block.vector
        def _(dve):
            def multiply(c, index):
                layer, t, n, (p, *_), _ = BODY[index]
                pair = index in PAIRED
                slots = products[0:p, index % RING, 0:n, :]
                if pair:
                    n += BODY[index + 1][2]
                    slots = products[0:p, index % RING:index % RING + 2, :, :].rearrange("p a b n -> p (a b) n")
                if layer == 0:
                    rep, row = x0_shifted[0:p, t:t + n, 0:N], x0_same[0:p, :]
                else:
                    rep, row = x0_rep[0:p, bass.ds(c % 2 * T1 + t, n), :], xk[layer - 1][0:p, :]
                nc.vector.tensor_tensor(slots, rep, row.unsqueeze(1).broadcast_to([p, n, N]),
                                        ALU.mult).then_inc(made, 1 + pair)

            def logits01(c):
                dve.wait_ge(direct1_ready, c + 1)
                nc.vector.tensor_reduce(logit01[:, bass.ds(c * BC, BC)],
                                        direct01[:, :].rearrange("s (b d) -> s b d", d=D),
                                        axis=AX.X, op=ALU.add).then_inc(logit01_ready, 1)

            def logits2(c):
                dve.wait_ge(direct2_ready, c + 1)
                nc.vector.tensor_reduce(logit2[:, bass.ds(c * BC, BC)],
                                        direct2[:, :].rearrange("s (b d) -> s b d", d=D),
                                        axis=AX.X, op=ALU.add).then_inc(logit2_ready, 1)

            def make_low(c, index):
                if index in STACKS:
                    dve.wait_ge(stack_rounded, count("stacked", c, index))
                    at = STACKS.index(index)
                    nc.vector.tensor_tensor(stacks[HALF:128, at, :], products[0:HALF, index % RING, 1, :],
                                            stacks[0:HALF, at, :].bitcast(fp32), ALU.subtract).then_inc(stack_low, 1)
                else:
                    low_part(dve, nc.vector, c, index)

            def body(c, indices):
                late = []
                for index in indices:
                    layer, t, n, _, kind = BODY[index]
                    if layer == 1:
                        if t == 0:
                            dve.wait_ge(xk0_ready, c + 1)
                        for q in {t // QT, (t + n - 1 + 2 * (index in PAIRED)) // QT}:
                            dve.wait_ge(rep_loaded[q], 32 * (c + 1))
                    if layer == 0 and isinstance(c, int) and c == -1:
                        dve.wait_ge(same_loaded, 16)
                        dve.wait_ge(shifted_loaded[index - N1], 16)
                    elif layer == 0 and t == 0:
                        dve.wait_ge(l0_loaded, 16 * L0_LOADS * (c + 1))
                    if layer == 2 and t == 0:
                        while late:
                            make_low(c, late.pop(0))
                        dve.wait_ge(xk1_ready, c + 1)
                    if index - 1 not in PAIRED:
                        wait_slot(dve, c, index)
                        if index in PAIRED:
                            wait_slot(dve, c, index + 1)
                        multiply(c, index)
                    if kind in (LOW_DVE, STACKED):
                        late.append(index)
                    while late and late[0] <= index - LOW_LAG:
                        make_low(c, late.pop(0))
                    if index == 8 and not (isinstance(c, int) and c == 0):
                        logits2(c - 1)
                    if index == N1 + N0 + 4:
                        logits01(c)
                for index in late:
                    make_low(c, index)

            everything = range(len(BODY))
            dve.wait_ge(w0_loaded, 32)
            nc.vector.tensor_tensor(w0_sb, w0a_sb, w0b_sb, ALU.add).then_inc(w0_added, 1)
            dve.wait_ge(w0_added, 1)
            nc.vector.tensor_copy(w0_sb[0:F, 0, :], w0a_sb[0:F, 0, :]).then_inc(w0_folded, 1)
            dve.wait_ge(w0_folded, 1)
            for n_taken, index in enumerate(WEIGHT_ORDER):
                layer, t, n, (p, *_), kind = BODY[index]
                if index == 0:
                    dve.wait_ge(w1_loaded, 48)
                if index == N1 + N0:
                    dve.wait_ge(w2_loaded, 48)
                if index in WHOLES:
                    nc.vector.tensor_copy(w_whole[0:p, WHOLES.index(index), 0:n, :],
                                          w_sb[layer][0:p, t:t + n, :]).then_inc(w_copied, 1)
                else:
                    at = SPLIT.index(index)
                    dve.wait_ge(w_rounded, sum(i in SPLIT for i in WEIGHT_ORDER[:n_taken + 1]))
                    nc.vector.tensor_tensor(w_low[0:p, at, 0:n, :], w_sb[layer][0:p, t:t + n, :],
                                            w_high[0:p, at, 0:n, :].bitcast(fp32),
                                            ALU.subtract).then_inc(w_copied, 1)
            for at, index in enumerate(STACKS):
                layer, t = BODY[index][:2]
                dve.wait_ge(w_stack_rounded, at + 1)
                nc.vector.tensor_tensor(w_stack_low[:, at, :], w_sb[layer][0:HALF, t + 1, :],
                                        w_stack_high[0:HALF, at, :].bitcast(fp32), ALU.subtract) \
                    .then_inc(w_stack_made, 1)
            body(-1, LAYER0)
            body(0, everything)
            with dve.Fori(1, C - 1) as c:
                body(c, everything)
            body(C - 1, [i for i in everything if i not in LAYER0])
            logits2(C - 1)

        @block.tensor
        def _(pe):
            tiles = [T0, T1, T1]

            def contract(c, index):
                layer, t, n, partitions, kind = BODY[index]
                slot, out = index % RING, z[layer][:, :]
                if kind == STACKED:
                    at, stack = WHOLES.index(index), STACKS.index(index)
                    pe.wait_ge(made, count("all", c, index))
                    nc.tensor.matmul(out, w_whole[:, at, 0, :], products[:, slot, 0, :], start=False, stop=False)
                    pe.wait_ge(stack_low, count("stacked", c, index))
                    nc.tensor.matmul(out, w_stack_high[:, stack, :], stacks[:, stack, :], start=False, stop=False)
                    mm = nc.tensor.matmul(out, w_stack_low[:, stack, :], stacks[0:HALF, stack, :],
                                          start=False, stop=True)
                elif kind == WHOLE:
                    at = WHOLES.index(index)
                    pe.wait_ge(made, count("all", c, index))
                    for i, p in enumerate(partitions):
                        mm = nc.tensor.matmul(out, w_whole[0:p, at, i, :], products[0:p, slot, i, :],
                                              start=(t + i == 0), stop=(t + i == tiles[layer] - 1))
                else:
                    at, part = SPLIT.index(index), part_slot(index)
                    pe.wait_ge(rounded, count("split", c, index))
                    for i, p in enumerate(partitions):
                        nc.tensor.matmul(out, w_high[0:p, at, i, :], high[0:p, part, i, :],
                                         start=(t + i == 0), stop=False)
                        nc.tensor.matmul(out, w_low[0:p, at, i, :], high[0:p, part, i, :], start=False, stop=False)
                    pe.wait_ge(low_by[kind], count(kind, c, index))
                    for i, p in enumerate(partitions):
                        mm = nc.tensor.matmul(out, w_high[0:p, at, i, :], low[0:p, part, i, :],
                                              start=False, stop=(t + i == tiles[layer] - 1))
                mm.then_inc(used, 1)

            def body(c, indices):
                first = isinstance(c, int) and c == 0
                for index in indices:
                    layer, t = BODY[index][:2]
                    if t == 0 and layer == 0 and not (isinstance(c, int) and c < 0):
                        pe.wait_ge(direct0_ready, c + 1)
                    if t == 0 and layer == 1 and not first:
                        pe.wait_ge(direct1_ready, c)
                    if t == 0 and layer == 2 and not first:
                        pe.wait_ge(direct2_ready, c)
                    contract(c, index)

            everything = range(len(BODY))
            pe.wait_ge(w_copied, len(BODY))
            pe.wait_ge(w_stack_made, len(STACKS))
            pe.wait_ge(early_loaded, 32)
            pe.wait_ge(same_loaded, 16)
            for m in range(EARLY):
                nc.tensor.matmul(z_hidden1[m][:, :], early_wt1d[:, m * 128:(m + 1) * 128], early_dense,
                                 start=True, stop=False)
            body(-1, LAYER0)
            body(0, everything)
            with pe.Fori(1, C - 1) as c:
                body(c, everything)
            body(C - 1, range(N1))

            def add_logits(m, source, logits, cols, stop=False):
                return nc.tensor.matmul(z_hidden1[m][:, cols], wt1_sb[:, source, m * 128:(m + 1) * 128],
                                        logits[:, cols], start=False, stop=stop)

            before_last, of_last = slice(0, B - BC), slice(B - BC, B)
            pe.wait_ge(top_loaded, 16 * 5)
            pe.wait_ge(direct0_ready, C)
            for m in range(EARLY, H1 // 128):
                nc.tensor.matmul(z_hidden1[m][:, :], wt1d_sb[:, m * 128:(m + 1) * 128], dense_sb,
                                 start=True, stop=False)
            pe.wait_ge(logit01_ready, C - 1)
            pe.wait_ge(logit2_ready, C - 1)
            for m in range(H1 // 128):
                add_logits(m, 0, logit01, before_last)
                add_logits(m, 1, logit2, before_last)
            body(C - 1, range(N1 + N0, len(BODY)))
            pe.wait_ge(logit01_ready, C)
            for m in range(H1 // 128):
                add_logits(m, 0, logit01, of_last)
            pe.wait_ge(logit2_ready, C)
            for m in range(H1 // 128):
                add_logits(m, 1, logit2, of_last, stop=True).then_inc(hidden1_done, 1)
            for k in range(H1 // 128):
                pe.wait_ge(hidden1_ready, k + 1)
                for m in range(H2 // 128):
                    mm = nc.tensor.matmul(z_hidden2[m][:, :], wt2_sb[:, k, m * 128:(m + 1) * 128], hidden1[:, k, :],
                                          start=(k == 0), stop=(k == H1 // 128 - 1))
                    if k == H1 // 128 - 1:
                        mm.then_inc(hidden2_done, 1)
            for k in range(H2 // 128):
                pe.wait_ge(hidden2_ready, k + 1)
                mm = nc.tensor.matmul(z_y[0:1, :], wt3_sb[:, k:k + 1], hidden2[:, k, :],
                                      start=(k == 0), stop=(k == H2 // 128 - 1))
            mm.then_inc(y_done, 1)

        @block.scalar
        def _(act):
            act.dma_start(b0_sb[:, :], b0).then_inc(biases_loaded, 16)
            act.dma_start(bx0_sb[:, :], bx0).then_inc(biases_loaded, 16)
            act.dma_start(b1_sb[:, :], b1).then_inc(biases_loaded, 16)
            act.dma_start(bx1_sb[:, :], bx1).then_inc(biases_loaded, 16)
            act.dma_start(b2_sb[:, :], b2).then_inc(biases_loaded, 16)
            for staging, w, loaded in ((w1_sb, w1, w1_loaded), (w2_sb, w2, w2_loaded)):
                full = (T1 - 1) * S
                rows = w.rearrange("h k s -> (h k) s")
                act.dma_start(staging[:, 0:T1 - 1, :], rows[0:full, :].rearrange("(t p) s -> p t s", p=S)) \
                    .then_inc(loaded, 16)
                for e in range(2):
                    act.dma_start(staging[e * HALF:(e + 1) * HALF, T1 - 1, :],
                                  rows[full:full + HALF, :]).then_inc(loaded, 16)
            act.dma_start(early_dense, dense).then_inc(early_loaded, 16)
            act.dma_start(early_wt1d, wt1[256:256 + DENSE, :]).then_inc(early_loaded, 16)
            act.dma_start(bt1_sb[:, :], bt1).then_inc(biases_loaded, 16)
            act.dma_start(bt2_sb[:, :], bt2).then_inc(biases_loaded, 16)

            def relu(out, in_, bias):
                return nc.scalar.activation(out, in_, RELU, bias=bias)

            def round_high(c, index):
                _, _, n, (p, *_), _ = BODY[index]
                if index in STACKS:
                    at = STACKS.index(index)
                    if not (isinstance(c, int) and c == 0):
                        act.wait_ge(used, count("all", c - 1, index))
                    act.wait_ge(made, count("all", c, index))
                    nc.scalar.activation(stacks[0:HALF, at, :], products[0:HALF, index % RING, 1, :],
                                         ACT.Copy).then_inc(stack_rounded, 1)
                    return
                slot = part_slot(index)
                wait_part_slot(act, c, index)
                act.wait_ge(made, count("all", c, index))
                nc.scalar.activation(high[0:p, slot, 0:n, :], products[0:p, index % RING, 0:n, :],
                                     ACT.Copy).then_inc(rounded, 1)

            def after_layer0(c):
                act.wait_ge(used, count("all", c, N1 + N0 - 1))
                relu(xk[0][HALF:S, :], z[0][HALF:S, :], bx0_sb[HALF:S, :])
                relu(xk[0][0:HALF, :], z[0][HALF:S, :], bx0_sb[HALF:S, :]).then_inc(xk0_ready, 1)
                if not (isinstance(c, int) and c < 0):
                    act.wait_ge(logit01_ready, c + 1)
                relu(direct01[0:HALF, :], z[0][0:HALF, :], b0_sb[0:HALF, :]).then_inc(direct0_ready, 1)

            def after_layer1(c):
                act.wait_ge(used, count("all", c, N1 - 1))
                relu(xk[1][0:HALF, :], z[1][0:HALF, :], bx1_sb[0:HALF, :])
                relu(xk[1][HALF:S, :], z[1][0:HALF, :], bx1_sb[0:HALF, :]).then_inc(xk1_ready, 1)
                relu(direct01[HALF:S, :], z[1][HALF:S, :], b1_sb[HALF:S, :]).then_inc(direct1_ready, 1)

            def after_layer2(c, first=False):
                act.wait_ge(used, count("all", c, len(BODY) - 1))
                if not first:
                    act.wait_ge(logit2_ready, c)
                relu(direct2[:, :], z[2][:, :], b2_sb[:, :]).then_inc(direct2_ready, 1)

            def body(c):
                first, last = isinstance(c, int) and c == 0, isinstance(c, int) and c == C - 1
                gathers = not isinstance(c, int) or c < C - 2
                for index in range(len(BODY)):
                    if index == 20 and gathers:
                        act.wait_ge(gather_done, 16 * GB * (c + 3))
                        write_x0(act, c + 2)
                    if index == 4 and not first:
                        after_layer2(c - 1, first=isinstance(c, int) and c == 1)
                    if index == N1 + 2:
                        after_layer1(c)
                    if index == N1 + N0 + 4 and not last:
                        after_layer0(c)
                    if index in SPLIT + STACKS and not (last and index in LAYER0):
                        round_high(c, index)

            for n_taken, index in enumerate(WEIGHT_ORDER):
                layer, t, n, (p, *_), kind = BODY[index]
                if index == N1:
                    act.wait_ge(w0_folded, 1)
                if index == 0:
                    act.wait_ge(w1_loaded, 48)
                if index == N1 + N0:
                    act.wait_ge(w2_loaded, 48)
                if index in STACKS:
                    nc.scalar.activation(w_stack_high[:, STACKS.index(index), :], w_sb[layer][:, t + 1, :],
                                         ACT.Copy).then_inc(w_stack_rounded, 1)
                if index in SPLIT:
                    nc.scalar.activation(w_high[0:p, SPLIT.index(index), 0:n, :],
                                         w_sb[layer][0:p, t:t + n, :], ACT.Copy).then_inc(w_rounded, 1)
            act.wait_ge(biases_loaded, 16 * 7)
            for index in LAYER0:
                if index in SPLIT:
                    round_high(-1, index)
            after_layer0(-1)
            body(0)
            body(1)
            with act.Fori(2, C - 2) as c:
                body(c)
            body(C - 2)
            body(C - 1)
            after_layer2(C - 1)

            for m in range(H1 // 128):
                act.wait_ge(hidden1_done, m + 1)
                relu(hidden1[:, m, :], z_hidden1[m][:, :], bt1_sb[:, m:m + 1]).then_inc(hidden1_ready, 1)
            for m in range(H2 // 128):
                act.wait_ge(hidden2_done, m + 1)
                relu(hidden2[:, m, :], z_hidden2[m][:, :], bt2_sb[:, m:m + 1]).then_inc(hidden2_ready, 1)
            act.wait_ge(y_done, 1)
            nc.scalar.activation(y_sb, z_y[0:1, :], ACT.Copy).then_inc(y_ready, 1)


def kernel(**inputs):
    import numpy as _np
    import concourse.bacc as _bacc
    from concourse import mybir as _mybir
    from concourse.bass_utils import run_bass_kernel_spmd as _run

    a = {k: _np.asarray(v) for k, v in inputs.items()}
    batch = (_np.arange(C)[None, :, None] * BC + _np.arange(GR)[:, None, None] * GB + _np.arange(GB)[None, None, :])
    ids = a["ids"][batch % B]
    ids = ids.transpose(0, 3, 1, 2).reshape(GP, C * GB)
    starts = _np.concatenate([[0], _np.cumsum(SIZES)[:-1]]).astype(_np.int32)
    base = _np.tile(starts, GR).reshape(GP, 1)
    tables = _np.concatenate([a[f"tbl_{f}"] for f in range(F)], axis=0)
    shift = _np.arange(GR)[:, None, None] * T0 + _np.arange(T0)[None, None, :]
    k = _np.broadcast_to(_np.arange(F)[None, :, None], (GR, F, T0))
    other = (k + shift) % F
    order = _np.concatenate([_np.arange(HALF, S), _np.arange(HALF)])
    w0 = a["L0_rec_w0"][:, :, order]
    b0, b1 = a["L0_rec_b0"][order], a["L0_rec_b1"]
    arrays = {
        "ids": ids, "base": base, "tables": tables, "dense": a["dense_ctx"].T,
        "w0a": w0[k, other].reshape(GP, T0, S), "w0b": w0[other, k].reshape(GP, T0, S),
        "b0": b0.reshape(S, 1), "bx0": _np.tile(b0[HALF:], 2).reshape(S, 1),
        "w1": a["L0_rec_w1"], "b1": b1.reshape(S, 1), "bx1": _np.tile(b1[:HALF], 2).reshape(S, 1),
        "w2": a["L0_rec_w2"], "b2": a["L0_rec_b2"].reshape(S, 1),
        "wt1": a["W_top1"], "bt1": a["b_top1"].reshape(H1 // 128, 128).T,
        "wt2": a["W_top2"], "bt2": a["b_top2"].reshape(H2 // 128, 128).T,
        "wt3": a["W_top3"].reshape(H2 // 128, 128).T,
    }
    nc = _bacc.Bacc("TRN2", target_bir_lowering=False, num_devices=1)
    sent, args = {}, []
    for name, v in arrays.items():
        v = _np.ascontiguousarray(v)
        sent[f"in_{name}"] = v
        args.append(nc.dram_tensor(f"in_{name}", v.shape, _mybir.dt.from_np(v.dtype), kind="ExternalInput").ap())
    args.append(nc.dram_tensor("out_y", (B, 1), _mybir.dt.float32, kind="ExternalOutput").ap())
    dlrm_cin_kernel(nc, *args)
    return _run(nc, [sent], core_ids=[0]).results[0]["out_y"]
```
